# Optimizing a Trainium2 kernel written in Bass

```python
import numpy as np
import jax
import jax.numpy as jnp

def _softmax(x, axis=-1):
    return jax.nn.softmax(x, axis=axis)

def _gelu(x):
    return jax.nn.gelu(x, approximate=True)

def _silu(x):
    return jax.nn.silu(x)

def _sigmoid(x):
    return jax.nn.sigmoid(x)

def _layernorm(x, axis=-1, eps=1e-05):
    m = jnp.mean(x, axis=axis, keepdims=True)
    v = jnp.var(x, axis=axis, keepdims=True)
    return (x - m) / jnp.sqrt(v + eps)

def _scatter_add(tgt, idx, src, axis=0):
    return tgt.at[idx].add(src)

def _segment_sum(src, seg, n):
    return jax.ops.segment_sum(src, seg, n)
kernel_name = 'mk_seq_preln_d1_jaxref_r8_5f08cf'

def setup_inputs(seed: int=0):
    np.random.seed(seed)
    _w = jnp.asarray

    def _L0_attn_setup():
        import jax, jax.numpy as jnp
        import numpy as np
        B, L, D_MODEL = (4, 256, 128)
        N_HEADS = 8
        D_HEAD = D_MODEL // N_HEADS
        D_INNER = 2 * D_HEAD
        D_STATE = 16
        D_CONV = 4
        DT_RANK = (D_HEAD + 15) // 16

        def _parallel_ssm(x, W_in, conv_w, conv_b, W_xp, W_dt, b_dt, A_log, Dp, W_out):
            b, l, dm = x.shape
            h = W_in.shape[0]
            dh = dm // h
            di = W_in.shape[-1] // 2
            n = A_log.shape[-1]
            r = W_dt.shape[1]
            k = conv_w.shape[-1]
            xh = x.reshape(b, l, h, dh)
            xz = jnp.einsum('blhd,hde->blhe', xh, W_in)
            xin, z = (xz[..., :di], xz[..., di:])
            xp = jnp.pad(xin, ((0, 0), (k - 1, 0), (0, 0), (0, 0)))
            conv = conv_b[None, None]
            for j in range(k):
                conv = conv + conv_w[None, None, :, :, j] * xp[:, j:j + l]
            xc = jax.nn.silu(conv)
            x_dbl = jnp.einsum('blhd,hde->blhe', xc, W_xp)
            dtr = x_dbl[..., :r]
            Bm = x_dbl[..., r:r + n]
            Cm = x_dbl[..., r + n:]
            dt = jax.nn.softplus(jnp.einsum('blhr,hrd->blhd', dtr, W_dt) + b_dt)
            A = -jnp.exp(A_log)

            def step(hstate, inp):
                dt_t, B_t, C_t, x_t = inp
                dA = jnp.exp(dt_t[..., None] * A)
                dBx = dt_t[..., None] * B_t[:, :, None, :] * x_t[..., None]
                hstate = dA * hstate + dBx
                y_t = jnp.einsum('bhdn,bhn->bhd', hstate, C_t)
                return (hstate, y_t)
            to_seq = lambda t: jnp.moveaxis(t, 1, 0)
            h0 = jnp.zeros((b, h, di, n), x.dtype)
            _, ys = jax.lax.scan(step, h0, (to_seq(dt), to_seq(Bm), to_seq(Cm), to_seq(xc)))
            y = jnp.moveaxis(ys, 0, 1)
            y = y + Dp * xc
            y = y * jax.nn.silu(z)
            out = jnp.einsum('blhe,hed->blhd', y, W_out)
            return out.reshape(b, l, dm)
        key = jax.random.key(seed)
        ks = jax.random.split(key, 8)
        s_in = 1.0 / np.sqrt(D_HEAD)
        s_x = 1.0 / np.sqrt(D_INNER)
        s_dt = 1.0 / np.sqrt(DT_RANK)
        x = jax.random.normal(ks[0], (B, L, D_MODEL), jnp.float32)
        W_in = jax.random.normal(ks[1], (N_HEADS, D_HEAD, 2 * D_INNER), jnp.float32) * s_in
        conv_w = jax.random.normal(ks[2], (N_HEADS, D_INNER, D_CONV), jnp.float32) * 0.5
        conv_b = jnp.zeros((N_HEADS, D_INNER), jnp.float32)
        W_xp = jax.random.normal(ks[3], (N_HEADS, D_INNER, DT_RANK + 2 * D_STATE), jnp.float32) * s_x
        W_dt = jax.random.normal(ks[4], (N_HEADS, DT_RANK, D_INNER), jnp.float32) * s_dt
        b_dt = jax.random.uniform(ks[5], (N_HEADS, D_INNER), jnp.float32, -4.0, -2.0)
        A_log = jnp.log(jnp.broadcast_to(jnp.arange(1, D_STATE + 1, dtype=jnp.float32), (N_HEADS, D_INNER, D_STATE)))
        Dp = jnp.ones((N_HEADS, D_INNER), jnp.float32)
        W_out = jax.random.normal(ks[6], (N_HEADS, D_INNER, D_HEAD), jnp.float32) * s_x
        return {'x': x, 'W_in': W_in, 'conv_w': conv_w, 'conv_b': conv_b, 'W_xp': W_xp, 'W_dt': W_dt, 'b_dt': b_dt, 'A_log': A_log, 'Dp': Dp, 'W_out': W_out}
    _L0_attn_in = _L0_attn_setup()

    def _L0_ffn_setup():
        import jax, jax.numpy as jnp
        import numpy as np
        B, T, D, E, K = (2, 256, 128, 8, 2)
        H = 2 * D
        key = jax.random.key(seed)
        ks = jax.random.split(key, 5)
        s = 0.02
        return {'x': jax.random.normal(ks[0], (B, T, D), jnp.float32), 'Wr': jax.random.normal(ks[1], (D, E), jnp.float32) * s, 'br': jnp.zeros((E,), jnp.float32), 'W1': jax.random.normal(ks[2], (E, D, H), jnp.float32) * s, 'b1': jnp.zeros((E, H), jnp.float32), 'W2': jax.random.normal(ks[3], (E, H, D), jnp.float32) * s, 'b2': jnp.zeros((E, D), jnp.float32)}
    _L0_ffn_in = _L0_ffn_setup()
    _d = {'L0_attn_x': _L0_attn_in['x'], 'L0_attn_W_in': _L0_attn_in['W_in'], 'L0_attn_conv_w': _L0_attn_in['conv_w'], 'L0_attn_conv_b': _L0_attn_in['conv_b'], 'L0_attn_W_xp': _L0_attn_in['W_xp'], 'L0_attn_W_dt': _L0_attn_in['W_dt'], 'L0_attn_b_dt': _L0_attn_in['b_dt'], 'L0_attn_A_log': _L0_attn_in['A_log'], 'L0_attn_Dp': _L0_attn_in['Dp'], 'L0_attn_W_out': _L0_attn_in['W_out'], 'L0_ffn_Wr': _L0_ffn_in['Wr'], 'L0_ffn_br': _L0_ffn_in['br'], 'L0_ffn_W1': _L0_ffn_in['W1'], 'L0_ffn_b1': _L0_ffn_in['b1'], 'L0_ffn_W2': _L0_ffn_in['W2'], 'L0_ffn_b2': _L0_ffn_in['b2']}
    _x0 = _d['L0_attn_x']
    _d['L0_attn_x'] = jax.random.normal(jax.random.fold_in(jax.random.key(seed), 1), (4, 1024, 128), dtype=_x0.dtype)
    del _x0
    return _d

def reference(L0_attn_x, L0_attn_W_in, L0_attn_conv_w, L0_attn_conv_b, L0_attn_W_xp, L0_attn_W_dt, L0_attn_b_dt, L0_attn_A_log, L0_attn_Dp, L0_attn_W_out, L0_ffn_Wr, L0_ffn_br, L0_ffn_W1, L0_ffn_b1, L0_ffn_W2, L0_ffn_b2):

    def _L0_attn_ref(x, W_in, conv_w, conv_b, W_xp, W_dt, b_dt, A_log, Dp, W_out):
        import jax, jax.numpy as jnp
        import numpy as np
        B, L, D_MODEL = (4, 256, 128)
        N_HEADS = 8
        D_HEAD = D_MODEL // N_HEADS
        D_INNER = 2 * D_HEAD
        D_STATE = 16
        D_CONV = 4
        DT_RANK = (D_HEAD + 15) // 16

        def _parallel_ssm(x, W_in, conv_w, conv_b, W_xp, W_dt, b_dt, A_log, Dp, W_out):
            b, l, dm = x.shape
            h = W_in.shape[0]
            dh = dm // h
            di = W_in.shape[-1] // 2
            n = A_log.shape[-1]
            r = W_dt.shape[1]
            k = conv_w.shape[-1]
            xh = x.reshape(b, l, h, dh)
            xz = jnp.einsum('blhd,hde->blhe', xh, W_in)
            xin, z = (xz[..., :di], xz[..., di:])
            xp = jnp.pad(xin, ((0, 0), (k - 1, 0), (0, 0), (0, 0)))
            conv = conv_b[None, None]
            for j in range(k):
                conv = conv + conv_w[None, None, :, :, j] * xp[:, j:j + l]
            xc = jax.nn.silu(conv)
            x_dbl = jnp.einsum('blhd,hde->blhe', xc, W_xp)
            dtr = x_dbl[..., :r]
            Bm = x_dbl[..., r:r + n]
            Cm = x_dbl[..., r + n:]
            dt = jax.nn.softplus(jnp.einsum('blhr,hrd->blhd', dtr, W_dt) + b_dt)
            A = -jnp.exp(A_log)

            def step(hstate, inp):
                dt_t, B_t, C_t, x_t = inp
                dA = jnp.exp(dt_t[..., None] * A)
                dBx = dt_t[..., None] * B_t[:, :, None, :] * x_t[..., None]
                hstate = dA * hstate + dBx
                y_t = jnp.einsum('bhdn,bhn->bhd', hstate, C_t)
                return (hstate, y_t)
            to_seq = lambda t: jnp.moveaxis(t, 1, 0)
            h0 = jnp.zeros((b, h, di, n), x.dtype)
            _, ys = jax.lax.scan(step, h0, (to_seq(dt), to_seq(Bm), to_seq(Cm), to_seq(xc)))
            y = jnp.moveaxis(ys, 0, 1)
            y = y + Dp * xc
            y = y * jax.nn.silu(z)
            out = jnp.einsum('blhe,hed->blhd', y, W_out)
            return out.reshape(b, l, dm)
        return _parallel_ssm(x, W_in, conv_w, conv_b, W_xp, W_dt, b_dt, A_log, Dp, W_out)

    def _L0_ffn_ref(x, Wr, br, W1, b1, W2, b2):
        import jax, jax.numpy as jnp
        import numpy as np
        B, T, D, E, K = (2, 256, 128, 8, 2)
        H = 2 * D
        logits = jnp.einsum('btd,de->bte', x, Wr) + br
        topv, topi = jax.lax.top_k(logits, K)
        sel_mask = jax.nn.one_hot(topi, E, dtype=logits.dtype).sum(-2) > 0
        neg_inf = jnp.finfo(logits.dtype).min
        gates = jax.nn.softmax(jnp.where(sel_mask, logits, neg_inf), axis=-1)
        h = jax.nn.relu(jnp.einsum('btd,edh->bteh', x, W1) + b1)
        out = jnp.einsum('bte,bteh,ehd->btd', gates, h, W2)
        out = out + jnp.einsum('bte,ed->btd', gates, b2)
        return out
    x = L0_attn_x
    x = x + _L0_attn_ref(_layernorm(x, axis=-1), L0_attn_W_in, L0_attn_conv_w, L0_attn_conv_b, L0_attn_W_xp, L0_attn_W_dt, L0_attn_b_dt, L0_attn_A_log, L0_attn_Dp, L0_attn_W_out)
    x = x + _L0_ffn_ref(_layernorm(x, axis=-1), L0_ffn_Wr, L0_ffn_br, L0_ffn_W1, L0_ffn_b1, L0_ffn_W2, L0_ffn_b2)
    return x

_drawn_inputs = setup_inputs


def setup_inputs(seed=0):
    import zlib

    import numpy as np

    out = dict(_drawn_inputs(seed))
    spreads = {'L0_attn_conv_b': (0.0, 0.1),
     'L0_attn_Dp': (1.0, 0.2),
     'L0_ffn_br': (0.0, 0.1),
     'L0_ffn_b1': (0.0, 0.593),
     'L0_ffn_b2': (0.0, 0.1)}
    factors = {}
    for name, (base, spread) in spreads.items():
        noise = np.random.default_rng([zlib.crc32(name.encode()), seed]).standard_normal(out[name].shape)
        drawn = base * np.exp(spread * noise) if base else spread * noise
        out[name] = jnp.asarray(drawn.astype(out[name].dtype))
    for name, factor in factors.items():
        out[name] = (out[name] * factor).astype(out[name].dtype)
    return out
```

```python
from contextlib import ExitStack

import concourse.bass as bass
from concourse import mybir

F32 = mybir.dt.float32
BF16 = mybir.dt.bfloat16
ALU = mybir.AluOpType
ACT = mybir.ActivationFunctionType
AX_X = mybir.AxisListType.X

P = 128
H = 8
DH = P // H
NT, NS, NQ = 2, 4, 4
DI = NT * NS * NQ
DT = NS * NQ
N = 16
E = 8
HID = 256
TOK = 512
SEQ = 1024
TT = TOK // P
TAPS = 4
EPS = 1e-5
XP = 1 + 2 * N
RING = 8
SHIFT = 2
LOOK = 3
BIG = 3.0e38

K_ID, K_SEL, K_YSEL = 0, 128, 128 + NQ * P
K_HM1 = K_YSEL + NQ * 32
K_HM2 = K_HM1 + H
K_ORD = K_HM2 + H
K_END = K_ORD + TT * E
C_CW, C_CB = 0, NT * TAPS
C_XP = C_CB + NT
C_BDT = C_XP + NT * XP
C_DP = C_BDT + NT
C_WO = C_DP + NT
C_END = C_WO + NT * DH


def channel(i):
    return i // DT, i % DT // NS, i % NS


def build(nc, x, consts, chan, w_in, w_dt, a_log, w_r, b_r, w_1, b_1, w_2, b_2, out):
    n_chunks = x.shape[0] // TOK
    n_pairs = n_chunks // 2
    ctx = ExitStack()
    with ctx:
        def sb(name, shape, dt=F32):
            return ctx.enter_context(nc.sbuf_tensor(name, shape, dt))

        def sem(name):
            return ctx.enter_context(nc.semaphore(name))

        cst = sb("cst", [P, K_END])
        chn = sb("chn", [P, C_END])
        win_c = sb("win_c", [P, 4 * DT])
        wdt_b = sb("wdt_b", [P, NT * DT * H])
        alog = sb("alog", [P, DI])
        neg_a = sb("neg_a", [P, DI])
        pos_a = sb("pos_a", [P, DI])
        wr = sb("wr", [P, E])
        br = sb("br", [1, E])
        w1 = sb("w1", [P, E, HID])
        b1 = sb("b1", [P, E * 2])
        w2 = sb("w2", [P, E, 2, P])
        b2 = sb("b2", [E, P])
        sel = sb("sel", [96, NQ, P], BF16)
        win = sb("win", [P, 4 * DT, H])
        wbc = sb("wbc", [P, 2, NT, H, N])
        wdt = sb("wdt", [P, NT, NT, DT, H])
        wout = sb("wout", [P, NT, H, DH])
        ones = sb("ones", [1, P])
        minus_half = sb("minus_half", [P, TT])
        xt = sb("xt", [P, TT, P])
        st6 = sb("st6", [P, TT, 6])
        mv = sb("mv", [P, TT, 2])
        rstd = sb("rstd", [P, TT])
        var = sb("var", [P, TT])
        xn = sb("xn", [P, TT, P])
        xnT = sb("xnT", [P, TOK])
        xin = sb("xin", [P, NT, TOK + TAPS - 1])
        cv = sb("cv", [P, NT, TOK])
        xc = sb("xc", [P, 2, NT, TOK])
        sz = sb("sz", [P, 2, NT, TOK])
        bc = sb("bc", [P, 2, 2, TOK])
        soft = sb("soft", [P, TOK])
        val = sb("val", [P, 2, NT, TOK])
        pieces = sb("pieces", [P, 3, 2, NT, TOK], BF16)
        stack = sb("stack", [96, 2, NS, 2, NT, TOK], BF16)
        decay = sb("decay", [P, RING, TOK])
        drive = sb("drive", [P, 4, TOK])
        state = sb("state", [P, RING, TOK])
        prod = sb("prod", [P, RING, TOK])
        carry = sb("carry", [P, DI])
        yg = sb("yg", [P, NT, TOK])
        xres = sb("xres", [P, TT, P])
        x2 = sb("x2", [P, TT, P])
        st6c = sb("st6c", [P, TT, 6])
        mvc = sb("mvc", [P, TT, 2])
        varc = sb("varc", [P, TT])
        rstdc = sb("rstdc", [P, TT])
        xn2 = sb("xn2", [P, TT, P])
        xn2T = sb("xn2T", [P, TOK])
        lg = sb("lg", [P, TT, E])
        lg2 = sb("lg2", [P, TT, E])
        top = sb("top", [P, 2, TT])
        first = sb("first", [P, 2, TT])
        eq = sb("eq", [P, 2, TT, E])
        pick = sb("pick", [P, 2, TT, E])
        both = sb("both", [P, TT, E])
        shifted = sb("shifted", [P, TT, E])
        expo = sb("expo", [P, TT, E])
        masked = sb("masked", [P, TT, E])
        total = sb("total", [P, TT])
        inv = sb("inv", [P, TT])
        gates = sb("gates", [P, TT, E])
        gT = sb("gT", [E, TOK])
        hid = sb("hid", [P, 2, 2, TOK])
        acc = sb("acc", [P, TT, P])

        ps_dt = [ctx.enter_context(nc.psum_tensor(f"ps_dt{i}", [P, TOK], F32)) for i in range(2)]
        ps_dx = [ctx.enter_context(nc.psum_tensor(f"ps_dx{i}", [P, TOK], F32)) for i in range(2)]
        ps_y = ctx.enter_context(nc.psum_tensor("ps_y", [P, TOK], F32))
        ps_a = ctx.enter_context(nc.psum_tensor("ps_a", [P, TOK], F32))
        ps_c = [ctx.enter_context(nc.psum_tensor(f"ps_c{i}", [P, TOK], F32)) for i in range(2)]

        ident = cst[:, K_ID:K_ID + P]
        ysel = cst[:, K_YSEL:K_YSEL + NQ * 32].rearrange("p (q m) -> p q m", q=NQ)
        head_of_in = cst[:, K_HM1:K_HM1 + H]
        head_of_ch = cst[:, K_HM2:K_HM2 + H]
        order = cst[:, K_ORD:K_ORD + TT * E].rearrange("p (t e) -> p t e", t=TT)
        wxp = chn[:, C_XP:C_XP + NT * XP].rearrange("p (t e) -> p t e", t=NT)

        s_w1 = sem("weights_small")
        s_w2 = sem("weights_ffn")
        s_sel = sem("sel_ready")
        s_wmix = sem("mixer_weights")
        s_apos = sem("a_positive")
        s_aneg = sem("a_ready")
        s_x = sem("x_loaded")
        s_st = sem("a_stats")
        s_rs = sem("a_rstd")
        s_xn = sem("a_normalized")
        s_ta = sem("a_psum_full")
        s_xnT = sem("xnT_ready")
        s_pad = sem("pad_ready")
        s_xin = sem("xin_ready")
        s_cv = sem("conv_steps")
        s_sz = sem("z_silu")
        s_xc = sem("xc_silu")
        s_bc = sem("bc_ready")
        s_spa = sem("softplus_act")
        s_dt = sem("dt_ready")
        s_dx = sem("dtx_ready")
        s_pc = sem("pieces_act")
        s_re = sem("pieces_pool")
        s_sk = sem("stack_loaded")
        s_bdt = sem("dt_broadcast")
        s_bdx = sem("dtx_broadcast")
        s_de = sem("decay_ready")
        s_dr = sem("drive_ready")
        s_h = sem("state_ready")
        s_pr = sem("product_ready")
        s_ca = sem("carry_ready")
        s_y = sem("y_groups")
        s_ys = sem("y_skip")
        s_yg = sem("y_gated")
        s_xr = sem("xres_loaded")
        s_op = sem("out_projected")
        s_x2 = sem("x2_ready")
        s_st2 = sem("c_stats")
        s_rs2 = sem("c_rstd")
        s_xn2 = sem("c_normalized")
        s_t2 = sem("xn2_transposed")
        s_x2T = sem("xn2T_ready")
        s_lo = sem("router_full")
        s_rt = sem("routing_steps")
        s_ex = sem("router_exp")
        s_gt = sem("gates_transposed")
        s_gT = sem("gT_ready")
        s_b2 = sem("b2_full")
        s_ai = sem("acc_started")
        s_l1 = sem("hidden_full")
        s_re1 = sem("relu_ready")
        s_l2 = sem("expert_full")
        s_ad = sem("expert_added")
        s_ao = sem("acc_parts")
        s_out = sem("out_stored")
        R_STEPS = 18
        SMALL = 5
        FFN = 6
        NR = DI // NS

        block = ctx.enter_context(nc.Block())

        def steps(eng, step):
            step(0, None, None, 0)
            step(1, 0, None, 1)
            with eng.Fori(0, n_pairs - 1) as k:
                step(2 * k + 2, 2 * k + 1, 2 * k, 0)
                step(2 * k + 3, 2 * k + 2, 2 * k + 1, 1)
            step(None, n_chunks - 1, n_chunks - 2, 0)
            step(None, None, n_chunks - 1, 1)

        def nonneg(eng, s, value):
            if isinstance(value, int) and value <= 0:
                return
            eng.wait_ge(s, value)

        @block.sync
        def _(sp):
            sp.dma_start(cst[:, :], consts).then_inc(s_w1, 16)
            sp.dma_start(chn[:, :], chan).then_inc(s_w1, 16)
            sp.dma_start(win_c[:, :], w_in).then_inc(s_w1, 16)
            sp.dma_start(wdt_b[:, :], w_dt.partition_broadcast(P)).then_inc(s_w1, 16)
            sp.dma_start(alog[:, :], a_log).then_inc(s_w1, 16)
            sp.dma_start(w1[:, :, :], w_1.rearrange("e d h -> d e h")).then_inc(s_w2, 16)
            sp.dma_start(w2[:, :, :, :], w_2.rearrange("e (k h) d -> h e k d", h=P)).then_inc(s_w2, 16)
            sp.dma_start(wr[:, :], w_r).then_inc(s_w2, 16)
            sp.dma_start(br[:, :], b_r).then_inc(s_w2, 16)
            sp.dma_start(b1[:, :], b_1).then_inc(s_w2, 16)
            sp.dma_start(b2[:, :], b_2).then_inc(s_w2, 16)

            def load(dst, c, done):
                rows = x[bass.ds(c * TOK, TOK), :].rearrange("(t p) c -> p t c", p=P)
                sp.dma_start(dst[:, :, :], rows).then_inc(done, 16)

            def step(ca, cb, cc, par):
                if ca is not None:
                    nonneg(sp, s_bdx, DI * (ca - 1))
                    for piece in range(3):
                        if piece < 2:
                            sp.wait_ge(s_pc, 4 * ca + 2 * piece + 2)
                        else:
                            sp.wait_ge(s_re, 4 * ca + 4)
                        for s in range(NS):
                            sp.dma_start(stack[32 * piece:32 * piece + 32, par, s, :, :, :],
                                         pieces[32 * s:32 * s + 32, piece, :, :, :]).then_inc(s_sk, 16)
                if cc is not None:
                    sp.wait_ge(s_ad, 1 + E * (cc + 1))
                    rows = out[bass.ds(cc * TOK, TOK), :].rearrange("(t p) c -> p t c", p=P)
                    sp.dma_start(rows, acc[:, :, :]).then_inc(s_out, 16)
                    sp.wait_ge(s_out, 16 * (cc + 1))
                    if not (isinstance(cc, int) and cc == n_chunks - 1):
                        load(xres, cc + 1, s_xr)
                elif cb is not None:
                    load(xres, 0, s_xr)

            steps(sp, step)

        @block.gpsimd
        def _(pool):
            def product(c, i, par):
                n = DI * c + i
                pool.wait_ge(s_h, n + 1)
                if i % NS == 0:
                    nonneg(pool, s_y, NR * c + i // NS - 1)
                if i == 0:
                    pool.wait_ge(s_bc, 2 * c + 2)
                pool.tensor_tensor(prod[:, n_mod(i), :], state[:, n_mod(i), :], bc[:, par, 1, :],
                                   ALU.mult).then_inc(s_pr, 1)

            def step(ca, cb, cc, par):
                bpar = 1 - par
                for i in range(DI):
                    j = i - SHIFT
                    if cb is not None:
                        product(cb, i, bpar)
                        if bpar == 0 and i % NS == NS - 1:
                            g = i // NS
                            r = n_mod(i - NS + 1)
                            pool.tensor_copy(carry[:, NS * g:NS * g + NS],
                                             state[:, r:r + NS, TOK - 1]).then_inc(s_ca, 1)
                        if i == 20:
                            gate(cb, 0, bpar)
                    if ca is not None:
                        if j == 1:
                            pool.wait_ge(s_st, 9 * ca + 9)
                            pool.tensor_tensor(rstd[:, :], var[:, :], minus_half[:, :], ALU.pow).then_inc(s_rs, 1)
                        if j == 17:
                            pool.wait_ge(s_dt, 2 * ca + 2)
                            nonneg(pool, s_re, 4 * ca)
                            pool.tensor_tensor(val[:, 1, :, :], val[:, 0, :, :], xc[:, par, :, :],
                                               ALU.mult).then_inc(s_dx, 1)
                        if j in (18, 19):
                            w = j - 18
                            if w == 0:
                                pool.wait_ge(s_dx, ca + 1)
                            pool.wait_ge(s_pc, 4 * ca + w + 1)
                            pool.tensor_tensor(val[:, w, :, :], val[:, w, :, :], pieces[:, 0, w, :, :],
                                               ALU.subtract).then_inc(s_re, 1)
                        if j in (21, 22):
                            w = j - 21
                            pool.wait_ge(s_re, 4 * ca + w + 1)
                            pool.wait_ge(s_pc, 4 * ca + 2 + w + 1)
                            pool.tensor_tensor(pieces[:, 2, w, :, :], val[:, w, :, :], pieces[:, 1, w, :, :],
                                               ALU.subtract).then_inc(s_re, 1)
                    if cc is not None:
                        if i == 2:
                            gate(cc, 1, par)
                        if i == 6:
                            pool.wait_ge(s_st2, 9 * cc + 9)
                            pool.tensor_tensor(rstdc[:, :], varc[:, :], minus_half[:, :], ALU.pow).then_inc(s_rs2, 1)

            def gate(c, T, par):
                pool.wait_ge(s_ys, 2 * c + T + 1)
                pool.wait_ge(s_sz, 2 * c + 2)
                pool.tensor_tensor(yg[:, T, :], yg[:, T, :], sz[:, par, T, :], ALU.mult).then_inc(s_yg, 1)

            pool.wait_ge(s_sel, 1)
            steps(pool, step)

        @block.scalar
        def _(act):
            act.wait_ge(s_w1, 16 * SMALL)
            act.preload_act_table_set("natural_log_exp_and_others")
            act.activation(pos_a[:, :], alog[:, :], ACT.Exp).then_inc(s_apos, 1)

            def decays(c, i):
                n = DI * c + i
                T, q, s = channel(i)
                d = DT * T + NQ * s + q
                act.wait_ge(s_bdt, n + 1)
                nonneg(act, s_h, n - RING + 1)
                act.activation(decay[:, n_mod(i), :], ps_dt[i % 2][:, :], ACT.Exp,
                               scale=neg_a[:, d:d + 1]).then_inc(s_de, 1)

            def a_copy(dst, job, c, done):
                act.wait_ge(s_ta, 9 * c + job + 1)
                act.activation(dst, ps_a[:, :], ACT.Copy).then_inc(done, 1)

            def softplus(c, T):
                act.wait_ge(s_ta, 9 * c + 7 + T + 1)
                if T == 0:
                    nonneg(act, s_re, 4 * c)
                act.activation(val[:, 0, T, :], ps_a[:, :], ACT.Identity,
                               bias=chn[:, C_BDT + T:C_BDT + T + 1]).then_inc(s_spa, 1)
                act.wait_ge(s_spa, 8 * c + 4 * T + 1)
                nonneg(act, s_dt, 2 * c + T)
                act.activation(soft[:, :], val[:, 0, T, :], ACT.Abs).then_inc(s_spa, 1)
                act.wait_ge(s_spa, 8 * c + 4 * T + 2)
                act.activation(soft[:, :], soft[:, :], ACT.Exp, scale=-1.0).then_inc(s_spa, 1)
                act.wait_ge(s_spa, 8 * c + 4 * T + 3)
                act.activation(soft[:, :], soft[:, :], ACT.Ln, bias=1.0).then_inc(s_spa, 1)

            def relu(c, e, half):
                act.wait_ge(s_l1, 2 * E * c + 2 * e + half + 1)
                if e >= 2:
                    act.wait_ge(s_l2, E * c + e - 1)
                act.activation(hid[:, e % 2, half, :], ps_c[l1_bank(e, half)][:, :], ACT.Relu,
                               bias=b1[:, 2 * e + half:2 * e + half + 1]).then_inc(s_re1, 1)

            def step(ca, cb, cc, par):
                if ca is not None:
                    nonneg(act, s_xn, TT * ca)
                    rows = x[bass.ds(ca * TOK, TOK), :].rearrange("(t p) c -> p t c", p=P)
                    act.dma_start(xt[:, :, :], rows).then_inc(s_x, 16)
                for i in range(DI):
                    j = i - SHIFT
                    if cb is not None:
                        if i == 0:
                            decays(cb, 0)
                        if i + 1 < DI:
                            decays(cb, i + 1)
                    if ca is not None:
                        if j == 3:
                            a_copy(xnT[:, :], 0, ca, s_xnT)
                        if j == 4:
                            act.wait_ge(s_pad, ca + 1)
                            a_copy(xin[:, 0, TAPS - 1:], 1, ca, s_xin)
                        if j == 5:
                            a_copy(xin[:, 1, TAPS - 1:], 2, ca, s_xin)
                        if j == 8:
                            for T in range(NT):
                                act.wait_ge(s_ta, 9 * ca + 3 + T + 1)
                                if T == 0:
                                    nonneg(act, s_yg, 2 * (ca - 1))
                                act.activation(sz[:, par, T, :], ps_a[:, :], ACT.Silu).then_inc(s_sz, 1)
                                act.wait_ge(s_cv, 8 * ca + 7 + T)
                                act.activation(xc[:, par, T, :], cv[:, T, :], ACT.Silu).then_inc(s_xc, 1)
                            act.preload_act_table_set("natural_log_exp_and_others")
                        if j == 10:
                            nonneg(act, s_pr, DI * (ca - 1))
                            a_copy(bc[:, par, 0, :], 5, ca, s_bc)
                        if j == 11:
                            a_copy(bc[:, par, 1, :], 6, ca, s_bc)
                        if j == 13:
                            softplus(ca, 0)
                        if j == 15:
                            softplus(ca, 1)
                        if j in (16, 18):
                            w = (j - 16) // 2
                            nonneg(act, s_sk, 16 * 12 * ca)
                            if w == 0:
                                act.wait_ge(s_dt, 2 * ca + 2)
                            else:
                                act.wait_ge(s_dx, ca + 1)
                            act.activation(pieces[:, 0, w, :, :], val[:, w, :, :], ACT.Copy).then_inc(s_pc, 1)
                        if j in (19, 20):
                            w = j - 19
                            act.wait_ge(s_re, 4 * ca + w + 1)
                            act.activation(pieces[:, 1, w, :, :], val[:, w, :, :], ACT.Copy).then_inc(s_pc, 1)
                    if cc is not None:
                        if i == 8:
                            act.wait_ge(s_t2, cc + 1)
                            act.activation(xn2T[:, :], ps_c[1][:, :], ACT.Copy).then_inc(s_x2T, 1)
                        if i == 9:
                            relu(cc, 0, 0)
                        if i == 10:
                            relu(cc, 0, 1)
                        if i == 13:
                            act.wait_ge(s_rt, R_STEPS * cc + 12)
                            act.activation(expo[:, :, :], shifted[:, :, :], ACT.Exp).then_inc(s_ex, 1)
                        if i == 15:
                            act.wait_ge(s_gt, cc + 1)
                            act.activation(gT[:, :], ps_c[1][0:E, :], ACT.Copy).then_inc(s_gT, 1)
                        if 17 <= i < 31:
                            e = 1 + (i - 17) // 2
                            relu(cc, e, (i - 17) % 2)

            act.wait_ge(s_aneg, 1)
            steps(act, step)

        @block.tensor
        def _(pe):
            pe.wait_ge(s_w1, 16 * SMALL)
            pe.wait_ge(s_sel, 1)
            pe.wait_ge(s_wmix, 1)

            def bcast(c, i, w, par):
                n = DI * c + i
                T, q, s = channel(i)
                if w == 0:
                    nonneg(pe, s_de, n - 1)
                    bank, done = ps_dt[i % 2], s_bdt
                else:
                    nonneg(pe, s_dr, n - 1)
                    bank, done = ps_dx[i % 2], s_bdx
                pe.matmul(bank[:, :], sel[:, q, :], stack[:, par, s, w, T, :],
                          start=True, stop=True).then_inc(done, 1)

            def y_group(c, g):
                q = g % NQ
                pe.wait_ge(s_pr, DI * c + NS * g + NS)
                if q == 0:
                    nonneg(pe, s_ys, 2 * c + g // NQ)
                for s in range(NS):
                    mm = pe.matmul(ps_y[32 * s:32 * s + 32, :], ysel[:, q, :], prod[:, n_mod(NS * g + s), :],
                                   start=(q == 0), stop=(q == NQ - 1))
                mm.then_inc(s_y, 1)

            def project(weights, rhs):
                for j, (a, b) in enumerate(zip(weights, rhs)):
                    mm = pe.matmul(ps_a[:, :], a, b, start=(j == 0), stop=(j == len(weights) - 1))
                mm.then_inc(s_ta, 1)

            def stage_a(c, i, par):
                j = i - SHIFT
                xcs = [xc[:, par, T, :] for T in range(NT)]
                if j == 3:
                    nonneg(pe, s_spa, 8 * c)
                    pe.wait_ge(s_xn, TT * (c + 1))
                    for t in range(TT):
                        mm = pe.transpose(ps_a[:, t * P:(t + 1) * P], xn[:, t, :], ident)
                    mm.then_inc(s_ta, 1)
                if j == 4:
                    pe.wait_ge(s_xnT, c + 1)
                    project([win2[:, 0, :]], [xnT[:, :]])
                if j == 5:
                    pe.wait_ge(s_xin, 2 * c + 1)
                    project([win2[:, 1, :]], [xnT[:, :]])
                if j == 6:
                    pe.wait_ge(s_xin, 2 * c + 2)
                    project([win2[:, 2, :]], [xnT[:, :]])
                if j == 8:
                    pe.wait_ge(s_sz, 2 * c + 1)
                    project([win2[:, 3, :]], [xnT[:, :]])
                if j == 10:
                    pe.wait_ge(s_sz, 2 * c + 2)
                    pe.wait_ge(s_xc, 2 * c + 2)
                    project([wbc2[:, 0, T, :] for T in range(NT)], xcs)
                if j == 11:
                    pe.wait_ge(s_bc, 2 * c + 1)
                    project([wbc2[:, 1, T, :] for T in range(NT)], xcs)
                if j == 12:
                    pe.wait_ge(s_bc, 2 * c + 2)
                    project([wdt2[:, T, 0, :] for T in range(NT)], xcs)
                if j == 14:
                    pe.wait_ge(s_spa, 8 * c + 1)
                    project([wdt2[:, T, 1, :] for T in range(NT)], xcs)

            def hidden(c, e, half):
                bank = ps_c[l1_bank(e, half)]
                pe.matmul(bank[:, :], w1[:, e, half * P:(half + 1) * P], xn2T[:, :],
                          start=True, stop=True).then_inc(s_l1, 1)

            def expert_out(c, e):
                pe.wait_ge(s_re1, 2 * E * c + 2 * e + 2)
                bank = ps_c[l2_bank(e)]
                for t in range(TT):
                    for half in range(2):
                        mm = pe.matmul(bank[:, t * P:(t + 1) * P], hid[:, e % 2, half, t * P:(t + 1) * P],
                                       w2[:, e, half, :], start=(half == 0), stop=(half == 1))
                mm.then_inc(s_l2, 1)

            def stage_c(c, i):
                if i == 1:
                    y_group(c, NR - 1)
                if i == 4:
                    pe.wait_ge(s_yg, 2 * c + 2)
                    pe.wait_ge(s_ad, 1 + E * c)
                    for t in range(TT):
                        for T in range(NT):
                            mm = pe.matmul(ps_c[0][:, t * P:(t + 1) * P], yg[:, T, t * P:(t + 1) * P],
                                           wout2[:, T, :], start=(T == 0), stop=(T == NT - 1))
                    mm.then_inc(s_op, 1)
                if i == 7:
                    pe.wait_ge(s_xn2, TT * (c + 1))
                    for t in range(TT):
                        mm = pe.transpose(ps_c[1][:, t * P:(t + 1) * P], xn2[:, t, :], ident)
                    mm.then_inc(s_t2, 1)
                if i == 8:
                    pe.wait_ge(s_x2T, c + 1)
                    pe.wait_ge(s_x2, c + 1)
                    if isinstance(c, int):
                        pe.wait_ge(s_w2, 16 * FFN)
                    for t in range(TT):
                        cols = ps_c[0][:, t * E:(t + 1) * E]
                        pe.matmul(cols, xn2T[:, t * P:(t + 1) * P], wr[:, :], start=True, stop=False)
                        mm = pe.matmul(cols, ones[:, :], br[:, :], start=False, stop=True)
                    mm.then_inc(s_lo, 1)
                    hidden(c, 0, 0)
                if i == 9:
                    pe.wait_ge(s_rt, R_STEPS * c + 1)
                    hidden(c, 0, 1)
                if i == 14:
                    pe.wait_ge(s_rt, R_STEPS * (c + 1))
                    pe.wait_ge(s_re1, 2 * E * c + 1)
                    for t in range(TT):
                        mm = pe.matmul(ps_c[1][0:E, t * P:(t + 1) * P], gates[:, t, :], ident, start=True, stop=True)
                    mm.then_inc(s_gt, 1)
                if i == 15:
                    pe.wait_ge(s_gT, c + 1)
                    pe.wait_ge(s_re1, 2 * E * c + 2)
                    for t in range(TT):
                        mm = pe.matmul(ps_c[0][:, t * P:(t + 1) * P], gT[:, t * P:(t + 1) * P], b2[:, :],
                                       start=True, stop=True)
                    mm.then_inc(s_b2, 1)
                if 16 <= i < 30:
                    e = (i - 16) // 2
                    if i % 2 == 0:
                        if e >= 1:
                            pe.wait_ge(s_ad, 1 + E * c + e)
                        hidden(c, e + 1, 0)
                        if e == 0:
                            pe.wait_ge(s_ai, c + 1)
                        expert_out(c, e)
                    else:
                        pe.wait_ge(s_re1, 2 * E * c + 2 * (e + 1) + 1)
                        hidden(c, e + 1, 1)
                if i == 31:
                    pe.wait_ge(s_ad, 1 + E * c + E - 1)
                    expert_out(c, E - 1)

            def step(ca, cb, cc, par):
                bpar = 1 - par
                if cb is not None:
                    pe.wait_ge(s_sk, 16 * 12 * (cb + 1))
                    for i in range(LOOK):
                        bcast(cb, i, 0, bpar)
                    bcast(cb, 0, 1, bpar)
                for i in range(DI):
                    if cb is not None:
                        if i + LOOK < DI:
                            bcast(cb, i + LOOK, 0, bpar)
                        if i + 1 < DI:
                            bcast(cb, i + 1, 1, bpar)
                        if i >= 6 and (i - 6) % NS == 0:
                            y_group(cb, (i - 6) // NS)
                    if ca is not None:
                        stage_a(ca, i, par)
                    if cc is not None:
                        stage_c(cc, i)

            win2 = win[:, :, :].rearrange("p (m e) h -> p m (e h)", m=4)
            wbc2 = wbc[:, :, :, :, :].rearrange("p b t h n -> p b t (h n)")
            wdt2 = wdt[:, :, :, :, :].rearrange("p k t d h -> p k t (d h)")
            wout2 = wout[:, :, :, :].rearrange("p t h i -> p t (h i)")
            steps(pe, step)

        @block.vector
        def _(dve):
            dve.wait_ge(s_w1, 16 * SMALL)
            dve.memset(ones[:, :], 1.0)
            dve.memset(minus_half[:, :], -0.5)
            dve.tensor_copy(sel[:, :, :], cst[0:96, K_SEL:K_SEL + NQ * P].rearrange("p (q m) -> p q m", q=NQ)
                            ).then_inc(s_sel, 1)
            dve.tensor_tensor(win[:, :, :], win_c[:, :].unsqueeze(2).to_broadcast([P, 4 * DT, H]),
                              head_of_in.unsqueeze(1).to_broadcast([P, 4 * DT, H]), ALU.mult)
            for T in range(NT):
                for b in range(2):
                    dve.tensor_tensor(wbc[:, b, T, :, :],
                                      wxp[:, T, 1 + N * b:1 + N * b + N].unsqueeze(1).to_broadcast([P, H, N]),
                                      head_of_ch.unsqueeze(2).to_broadcast([P, H, N]), ALU.mult)
                for T2 in range(NT):
                    dve.scalar_tensor_tensor(
                        out=wdt[:, T, T2, :, :],
                        in0=wdt_b[:, T2 * DT * H:(T2 + 1) * DT * H].rearrange("p (d h) -> p d h", h=H),
                        scalar=wxp[:, T, 0:1], in1=head_of_ch.unsqueeze(1).to_broadcast([P, DT, H]),
                        op0=ALU.mult, op1=ALU.mult)
                last = dve.tensor_tensor(
                    wout[:, T, :, :],
                    chn[:, C_WO + T * DH:C_WO + (T + 1) * DH].unsqueeze(1).to_broadcast([P, H, DH]),
                    head_of_ch.unsqueeze(2).to_broadcast([P, H, DH]), ALU.mult)
            last.then_inc(s_wmix, 1)
            dve.wait_ge(s_apos, 1)
            dve.tensor_scalar(neg_a[:, :], pos_a[:, :], -1.0, None, ALU.mult).then_inc(s_aneg, 1)
            dve.wait_ge(s_aneg, 1)
            dve.memset(both[:, :, :], 0.0).then_inc(s_ad, 1)

            def drives(c, i, par):
                n = DI * c + i
                dve.wait_ge(s_bdx, n + 1)
                nonneg(dve, s_h, n - 3)
                dve.tensor_tensor(drive[:, i % 4, :], ps_dx[i % 2][:, :], bc[:, par, 0, :],
                                  ALU.mult).then_inc(s_dr, 1)

            def scan(c, i, par):
                n = DI * c + i
                dve.wait_ge(s_de, n + 1)
                dve.wait_ge(s_dr, n + 1)
                if i % NS == 0 and (i >= RING) == (par == 0):
                    nonneg(dve, s_pr, n - RING + NS + 1)
                else:
                    nonneg(dve, s_pr, n - RING + 1)
                initial = 0.0
                if par == 1:
                    if i % NS == 0:
                        dve.wait_ge(s_ca, carries(c, i))
                    initial = carry[:, i:i + 1]
                dve.tensor_tensor_scan(state[:, n_mod(i), :], decay[:, n_mod(i), :], drive[:, i % 4, :],
                                       initial, ALU.mult, ALU.add).then_inc(s_h, 1)

            def carries(c, i):
                return half(c, NR) + i // NS + 1

            def half(c, per):
                if isinstance(c, int):
                    return (c // 2) * per
                return (c - 1) * (per // 2)

            def stats(src, st, m, v, done, c, k):
                if k == 0:
                    for t in range(TT):
                        dve.bn_stats(st[:, t, :], src[:, t, :]).then_inc(done, 1)
                if k == 1:
                    for t in range(TT):
                        dve.bn_aggr(m[:, t, :], st[:, t, :]).then_inc(done, 1)
                if k == 2:
                    dve.wait_ge(done, 9 * c + 2 * TT)
                    dve.tensor_scalar(v[:, :], m[:, :, 1], EPS, None, ALU.add).then_inc(done, 1)

            def normalize(src, m, r, dst, done):
                for t in range(TT):
                    dve.tensor_scalar(dst[:, t, :], src[:, t, :], m[:, t, 0:1], r[:, t:t + 1],
                                      ALU.subtract, ALU.mult).then_inc(done, 1)

            def conv(c, k):
                for T in range(NT):
                    taps = chn[:, C_CW + TAPS * T + k:C_CW + TAPS * T + k + 1]
                    src = xin[:, T, k:k + TOK]
                    if k == 0:
                        dve.wait_ge(s_xin, 2 * c + T + 1)
                        if T == 0:
                            nonneg(dve, s_xc, 2 * c)
                        dve.tensor_scalar(cv[:, T, :], src, taps, chn[:, C_CB + T:C_CB + T + 1],
                                          ALU.mult, ALU.add).then_inc(s_cv, 1)
                    else:
                        dve.wait_ge(s_cv, 8 * c + 2 * k + T - 1)
                        dve.scalar_tensor_tensor(out=cv[:, T, :], in0=src, scalar=taps, in1=cv[:, T, :],
                                                 op0=ALU.mult, op1=ALU.add).then_inc(s_cv, 1)

            def softplus(c, T):
                dve.wait_ge(s_spa, 8 * c + 4 * T + 4)
                dve.scalar_tensor_tensor(out=val[:, 0, T, :], in0=val[:, 0, T, :], scalar=0.0, in1=soft[:, :],
                                         op0=ALU.max, op1=ALU.add).then_inc(s_dt, 1)

            def skip(c, T, par):
                dve.wait_ge(s_y, NR * c + NQ * (T + 1))
                if T == 0:
                    nonneg(dve, s_op, c)
                dve.scalar_tensor_tensor(out=yg[:, T, :], in0=xc[:, par, T, :],
                                         scalar=chn[:, C_DP + T:C_DP + T + 1], in1=ps_y[:, :],
                                         op0=ALU.mult, op1=ALU.add).then_inc(s_ys, 1)

            def over_e(ap):
                return ap.unsqueeze(2).to_broadcast([P, TT, E])

            def routing(c, k):
                base = R_STEPS * c
                if k > 0:
                    dve.wait_ge(s_rt, base + k)
                if k == 0:
                    dve.wait_ge(s_lo, c + 1)
                    op = dve.tensor_copy(lg[:, :, :], ps_c[0][:, 0:TT * E].rearrange("p (t e) -> p t e", t=TT))
                elif k == 1:
                    op = dve.tensor_reduce(top[:, 0, :], lg[:, :, :], AX_X, ALU.max)
                elif k == 2:
                    op = dve.tensor_tensor(eq[:, 0, :, :], lg[:, :, :], over_e(top[:, 0, :]), ALU.is_equal)
                elif k == 3:
                    op = dve.tensor_tensor(eq[:, 0, :, :], eq[:, 0, :, :], order, ALU.mult)
                elif k == 4:
                    op = dve.tensor_reduce(first[:, 0, :], eq[:, 0, :, :], AX_X, ALU.max)
                elif k == 5:
                    op = dve.tensor_tensor(pick[:, 0, :, :], eq[:, 0, :, :], over_e(first[:, 0, :]), ALU.is_equal)
                elif k == 6:
                    op = dve.scalar_tensor_tensor(out=lg2[:, :, :], in0=pick[:, 0, :, :], scalar=-BIG,
                                                  in1=lg[:, :, :], op0=ALU.mult, op1=ALU.add)
                elif k == 7:
                    op = dve.tensor_reduce(top[:, 1, :], lg2[:, :, :], AX_X, ALU.max)
                elif k == 8:
                    op = dve.tensor_tensor(eq[:, 1, :, :], lg2[:, :, :], over_e(top[:, 1, :]), ALU.is_equal)
                elif k == 9:
                    op = dve.tensor_tensor(eq[:, 1, :, :], eq[:, 1, :, :], order, ALU.mult)
                elif k == 10:
                    op = dve.tensor_reduce(first[:, 1, :], eq[:, 1, :, :], AX_X, ALU.max)
                elif k == 11:
                    op = dve.tensor_tensor(shifted[:, :, :], lg[:, :, :], over_e(top[:, 0, :]), ALU.subtract)
                elif k == 12:
                    op = dve.tensor_tensor(pick[:, 1, :, :], eq[:, 1, :, :], over_e(first[:, 1, :]), ALU.is_equal)
                elif k == 13:
                    op = dve.tensor_tensor(both[:, :, :], pick[:, 0, :, :], pick[:, 1, :, :], ALU.add)
                elif k == 14:
                    dve.wait_ge(s_ex, c + 1)
                    op = dve.tensor_tensor(masked[:, :, :], expo[:, :, :], both[:, :, :], ALU.mult)
                elif k == 15:
                    op = dve.tensor_reduce(total[:, :], masked[:, :, :], AX_X, ALU.add)
                elif k == 16:
                    op = dve.reciprocal(inv[:, :], total[:, :])
                elif k == 17:
                    op = dve.tensor_tensor(gates[:, :, :], masked[:, :, :], over_e(inv[:, :]), ALU.mult)
                op.then_inc(s_rt, 1)

            def add_expert(c, e):
                dve.wait_ge(s_l2, E * c + e + 1)
                if e > 0:
                    dve.wait_ge(s_ad, 1 + E * c + e)
                else:
                    dve.wait_ge(s_ai, c + 1)
                bank = ps_c[l2_bank(e)]
                for t in range(TT):
                    op = dve.scalar_tensor_tensor(out=acc[:, t, :], in0=bank[:, t * P:(t + 1) * P],
                                                  scalar=gates[:, t, e:e + 1], in1=acc[:, t, :],
                                                  op0=ALU.mult, op1=ALU.add)
                op.then_inc(s_ad, 1)

            def fill_a(c, i, k, par):
                j = i - SHIFT
                if j == 0 and k == 0:
                    dve.wait_ge(s_x, 16 * (c + 1))
                    stats(xt, st6, mv, var, s_st, c, 0)
                if j == 0 and k == 1:
                    stats(xt, st6, mv, var, s_st, c, 1)
                if j == 1 and k == 0:
                    stats(xt, st6, mv, var, s_st, c, 2)
                if j == 2 and k == 1:
                    dve.wait_ge(s_rs, c + 1)
                    nonneg(dve, s_ta, 9 * (c - 1) + 1)
                    normalize(xt, mv, rstd, xn, s_xn)
                if j == 3 and k == 0:
                    nonneg(dve, s_cv, 8 * c)
                    if par == 0:
                        dve.memset(xin[:, :, 0:TAPS - 1], 0.0).then_inc(s_pad, 1)
                    else:
                        dve.tensor_copy(xin[:, :, 0:TAPS - 1], xin[:, :, TOK:TOK + TAPS - 1]).then_inc(s_pad, 1)
                if j in (6, 7):
                    if j == 6 and k == 0:
                        dve.wait_ge(s_pad, c + 1)
                    conv(c, 2 * (j - 6) + k)
                if j in (14, 16) and k == 1:
                    softplus(c, (j - 14) // 2)

            def fill_c(c, i, k, par):
                if i == 2 and k == 0:
                    skip(c, 1, par)
                if i == 5:
                    if k == 0:
                        dve.wait_ge(s_op, c + 1)
                        dve.wait_ge(s_xr, 16 * (c + 1))
                        dve.tensor_tensor(x2[:, :, :], ps_c[0][:, :].rearrange("p (t d) -> p t d", t=TT),
                                          xres[:, :, :], ALU.add).then_inc(s_x2, 1)
                    else:
                        dve.wait_ge(s_x2, c + 1)
                        stats(x2, st6c, mvc, varc, s_st2, c, 0)
                if i == 6:
                    stats(x2, st6c, mvc, varc, s_st2, c, 1 + k)
                if i == 7 and k == 0:
                    dve.wait_ge(s_rs2, c + 1)
                    normalize(x2, mvc, rstdc, xn2, s_xn2)
                if 9 <= i < 9 + R_STEPS // 4:
                    routing(c, 4 * (i - 9) + 2 * k)
                    routing(c, 4 * (i - 9) + 2 * k + 1)
                if i == 13:
                    routing(c, 16 + k)
                if i == 16 and k == 0:
                    dve.wait_ge(s_b2, c + 1)
                    dve.tensor_tensor(acc[:, :, :], ps_c[0][:, :].rearrange("p (t d) -> p t d", t=TT),
                                      x2[:, :, :], ALU.add).then_inc(s_ai, 1)
                if 17 <= i < 31 and i % 2 == 1 and k == 1:
                    add_expert(c, (i - 17) // 2)
                if i == 31 and k == 1:
                    add_expert(c, E - 1)

            def step(ca, cb, cc, par):
                bpar = 1 - par
                if cb is not None:
                    dve.wait_ge(s_bc, 2 * cb + 1)
                    drives(cb, 0, bpar)
                for i in range(DI):
                    for k in range(2):
                        if ca is not None and (i, k) == (SHIFT, 1):
                            dve.wait_ge(s_st, 9 * ca + TT)
                        if cc is not None and (i, k) == (6, 0):
                            dve.wait_ge(s_st2, 9 * cc + TT)
                        if cb is not None:
                            if k == 0 and i + 1 < DI:
                                drives(cb, i + 1, bpar)
                            if k == 1:
                                scan(cb, i, bpar)
                                if i == 19:
                                    skip(cb, 0, bpar)
                        if cc is not None:
                            fill_c(cc, i, k, par)
                        if ca is not None:
                            fill_a(ca, i, k, par)

            steps(dve, step)


def n_mod(i):
    return i % RING


def l1_bank(e, half):
    job = (3, 4)[half] if e == 0 else (3 * e + 4, 3 * e + 6)[half]
    return job % 2


def l2_bank(e):
    return (3 * e + 8 if e < E - 1 else 28) % 2


def kernel(L0_attn_x, L0_attn_W_in, L0_attn_conv_w, L0_attn_conv_b, L0_attn_W_xp, L0_attn_W_dt,
           L0_attn_b_dt, L0_attn_A_log, L0_attn_Dp, L0_attn_W_out, L0_ffn_Wr, L0_ffn_br, L0_ffn_W1,
           L0_ffn_b1, L0_ffn_W2, L0_ffn_b2):
    import numpy as np
    import concourse.bacc as bacc
    from concourse.bass_utils import run_bass_kernel_spmd

    c = np.zeros((P, K_END), np.float32)
    rows = np.arange(P)
    c[rows, K_ID + rows] = 1
    for q in range(NQ):
        for h in range(H):
            for piece in range(3):
                c[32 * piece + 8 * q + h, K_SEL + P * q + N * h:K_SEL + P * q + N * h + N] = 1
            c[N * h:N * h + N, K_YSEL + 32 * q + 8 * q + h] = 1
    c[rows, K_HM1 + rows // DH] = 1
    c[rows, K_HM2 + rows % H] = 1
    c[:, K_ORD:K_END] = np.tile(np.arange(E, 0, -1), TT)

    def by_channel(a):
        a = np.asarray(a).reshape((H, NT, DT) + a.shape[2:])
        a = np.moveaxis(a, (2, 0, 1), (0, 1, 2))
        return np.ascontiguousarray(a).reshape(P, -1)

    chan = np.concatenate([by_channel(a) for a in (L0_attn_conv_w, L0_attn_conv_b, L0_attn_W_xp,
                                                   L0_attn_b_dt, L0_attn_Dp, L0_attn_W_out)], axis=1)
    arrays = {
        "x_in": np.ascontiguousarray(L0_attn_x).reshape(-1, P),
        "consts_in": c,
        "chan_in": chan,
        "w_in_in": np.ascontiguousarray(L0_attn_W_in).reshape(P, 4 * DT),
        "w_dt_in": np.ascontiguousarray(np.transpose(np.asarray(L0_attn_W_dt)[:, 0, :], (1, 0))).reshape(-1),
        "a_log_in": np.ascontiguousarray(np.transpose(np.asarray(L0_attn_A_log), (0, 2, 1))).reshape(P, DI),
        "w_r_in": np.ascontiguousarray(L0_ffn_Wr),
        "b_r_in": np.ascontiguousarray(L0_ffn_br).reshape(1, E),
        "w_1_in": np.ascontiguousarray(L0_ffn_W1),
        "b_1_in": np.ascontiguousarray(np.transpose(np.asarray(L0_ffn_b1).reshape(2 * E, P), (1, 0))),
        "w_2_in": np.ascontiguousarray(L0_ffn_W2),
        "b_2_in": np.ascontiguousarray(L0_ffn_b2),
    }
    nc = bacc.Bacc("TRN2", target_bir_lowering=False, num_devices=1)
    args = [nc.dram_tensor(name, a.shape, mybir.dt.from_np(a.dtype), kind="ExternalInput").ap()
            for name, a in arrays.items()]
    shape = tuple(L0_attn_x.shape)
    out = nc.dram_tensor("block_out", (shape[0] * shape[1], P), F32, kind="ExternalOutput").ap()
    build(nc, *args, out)
    r = run_bass_kernel_spmd(nc, [arrays], core_ids=[0])
    return np.asarray(r.results[0]["block_out"]).reshape(shape)
```

```python
from contextlib import ExitStack

import concourse.bass as bass
from concourse import mybir

F32 = mybir.dt.float32
BF16 = mybir.dt.bfloat16
ALU = mybir.AluOpType
ACT = mybir.ActivationFunctionType
AX_X = mybir.AxisListType.X

P = 128
H = 8
DH = P // H
NT, NS, NQ = 2, 4, 4
DI = NT * NS * NQ
DT = NS * NQ
N = 16
E = 8
HID = 256
TOK = 512
SEQ = 1024
TT = TOK // P
TAPS = 4
EPS = 1e-5
XP = 1 + 2 * N
RING = 8
LOOK = 3
BIG = 3.0e38
PE_AT = dict(turn=5, in0=7, in1=8, in2=9, in3=10, b=13, c=14, dt0=16, dt1=17, y=2, out=4, turn2=9,
             route=11, gates=19, bias=24)
ACT_AT = dict(xnT=7, xin0=7, xin1=8, z0=9, z1=13, silu=13, b=14, c=15, sp00=17, sp01=17, sp02=17,
              sp03=17, sp10=18, sp11=18, sp12=19, sp13=20, pc00=20, pc01=21, pc02=22, pc03=22,
              pc10=24, pc11=26, pc12=26, pc13=30, turn2=9, expo=15, gates=23)
DVE_AT = dict(stat0=2, stat1=4, stat2=5, norm=7, pad=8, conv0=17, conv1=18, conv2=21, conv3=21,
              dt0=35, dt1=44, skip0=39, skip1=4, x2=8, cstat0=9, cstat1=11, cstat2=12, norm2=14,
              bias=57)
POOL_AT = dict(rstd=1, mul0=17, mul1=22, re00=19, re01=19, re02=20, re03=22, re10=23, re11=25,
               re12=27, re13=30, gate0=23, gate1=1, rstd2=5)
ROUTE_AT = [19, 20, 21, 22, 22, 23, 24, 25, 25, 26, 26, 27, 29, 29, 32, 33, 34, 35]
HIDDEN_AT = [10, 11, 12, 12, 18, 20, 21, 22, 24, 24, 25, 26, 27, 29, 30, 31]
RELU_AT = [11, 11, 13, 16, 19, 21, 22, 24, 25, 25, 25, 26, 28, 29, 30, 31]
EXPERT_AT = [12, 17, 20, 20, 23, 23, 24, 24, 27, 27, 28, 28, 30, 30, 31, 31]
ADD_AT = [36, 43, 45, 49, 54, 58, 61, 63]
Y_AT = 6

K_ID, K_SEL, K_YSEL = 0, 128, 128 + NQ * P
K_HM1 = K_YSEL + NQ * 32
K_HM2 = K_HM1 + H
K_ORD = K_HM2 + H
K_END = K_ORD + TT * E
C_CW, C_CB = 0, NT * TAPS
C_XP = C_CB + NT
C_BDT = C_XP + NT * XP
C_DP = C_BDT + NT
C_WO = C_DP + NT
C_END = C_WO + NT * DH


def channel(i):
    return i // DT, i % DT // NS, i % NS


def build(nc, x, consts, chan, w_in, w_dt, a_log, w_r, b_r, w_1, b_1, w_2, b_2, out):
    n_chunks = x.shape[0] // TOK
    n_pairs = n_chunks // 2
    ctx = ExitStack()
    with ctx:
        def sb(name, shape, dt=F32):
            return ctx.enter_context(nc.sbuf_tensor(name, shape, dt))

        def sem(name):
            return ctx.enter_context(nc.semaphore(name))

        cst = sb("cst", [P, K_END])
        chn = sb("chn", [P, C_END])
        win_c = sb("win_c", [P, 4 * DT])
        wdt_b = sb("wdt_b", [P, NT * DT * H])
        alog = sb("alog", [P, DI])
        neg_a = sb("neg_a", [P, DI])
        pos_a = sb("pos_a", [P, DI])
        wr = sb("wr", [P, E])
        br = sb("br", [1, E])
        w1 = sb("w1", [P, E, HID])
        b1 = sb("b1", [P, E * 2])
        w2 = sb("w2", [P, E, 2, P])
        b2 = sb("b2", [E, P])
        sel = sb("sel", [96, NQ, P], BF16)
        win = sb("win", [P, 4 * DT, H])
        wbc = sb("wbc", [P, 2, NT, H, N])
        wdt = sb("wdt", [P, NT, NT, DT, H])
        wout = sb("wout", [P, NT, H, DH])
        ones = sb("ones", [1, P])
        minus_half = sb("minus_half", [P, TT])
        xt = sb("xt", [P, TT, P])
        st6 = sb("st6", [P, TT, 6])
        mv = sb("mv", [P, TT, 2])
        rstd = sb("rstd", [P, TT])
        var = sb("var", [P, TT])
        xn = sb("xn", [P, TT, P])
        xnT = sb("xnT", [P, TOK])
        xin = sb("xin", [P, NT, TOK + TAPS - 1])
        cv = sb("cv", [P, NT, TOK])
        xc = sb("xc", [P, 2, NT, TOK])
        sz = sb("sz", [P, 2, NT, TOK])
        bc = sb("bc", [P, 2, 2, TOK])
        soft = sb("soft", [P, TOK])
        val = sb("val", [P, 2, NT, TOK])
        pieces = sb("pieces", [P, NT, 3, 2, TOK], BF16)
        stack = sb("stack", [96, 2, NT, NS, 2, TOK], BF16)
        decay = sb("decay", [P, RING, TOK])
        drive = sb("drive", [P, 4, TOK])
        state = sb("state", [P, RING, TOK])
        prod = sb("prod", [P, RING, TOK])
        carry = sb("carry", [P, DI])
        yg = sb("yg", [P, NT, TOK])
        xres = sb("xres", [P, TT, P])
        x2 = sb("x2", [P, TT, P])
        st6c = sb("st6c", [P, TT, 6])
        mvc = sb("mvc", [P, TT, 2])
        varc = sb("varc", [P, TT])
        rstdc = sb("rstdc", [P, TT])
        xn2 = sb("xn2", [P, TT, P])
        xn2T = sb("xn2T", [P, TOK])
        lg = sb("lg", [P, TT, E])
        lg2 = sb("lg2", [P, TT, E])
        top = sb("top", [P, 2, TT])
        first = sb("first", [P, 2, TT])
        eq = sb("eq", [P, 2, TT, E])
        pick = sb("pick", [P, 2, TT, E])
        both = sb("both", [P, TT, E])
        shifted = sb("shifted", [P, TT, E])
        expo = sb("expo", [P, TT, E])
        masked = sb("masked", [P, TT, E])
        total = sb("total", [P, TT])
        inv = sb("inv", [P, TT])
        gates = sb("gates", [P, TT, E])
        gT = sb("gT", [E, TOK])
        hid = sb("hid", [P, 2, 2, TOK])
        acc = sb("acc", [P, TT, P])

        ps_dt = [ctx.enter_context(nc.psum_tensor(f"ps_dt{i}", [P, TOK], F32)) for i in range(2)]
        ps_dx = [ctx.enter_context(nc.psum_tensor(f"ps_dx{i}", [P, TOK], F32)) for i in range(2)]
        ps_y = ctx.enter_context(nc.psum_tensor("ps_y", [P, TOK], F32))
        ps_a = ctx.enter_context(nc.psum_tensor("ps_a", [P, TOK], F32))
        ps_c = [ctx.enter_context(nc.psum_tensor(f"ps_c{i}", [P, TOK], F32)) for i in range(2)]

        ident = cst[:, K_ID:K_ID + P]
        ysel = cst[:, K_YSEL:K_YSEL + NQ * 32].rearrange("p (q m) -> p q m", q=NQ)
        head_of_in = cst[:, K_HM1:K_HM1 + H]
        head_of_ch = cst[:, K_HM2:K_HM2 + H]
        order = cst[:, K_ORD:K_ORD + TT * E].rearrange("p (t e) -> p t e", t=TT)
        wxp = chn[:, C_XP:C_XP + NT * XP].rearrange("p (t e) -> p t e", t=NT)

        s_w1 = sem("weights_small")
        s_w2 = sem("weights_ffn")
        s_sel = sem("sel_ready")
        s_wmix = sem("mixer_weights")
        s_apos = sem("a_positive")
        s_aneg = sem("a_ready")
        s_x = sem("x_loaded")
        s_st = sem("a_stats")
        s_rs = sem("a_rstd")
        s_xn = sem("a_normalized")
        s_ta = sem("a_psum_full")
        s_xnT = sem("xnT_ready")
        s_pad = sem("pad_ready")
        s_xin = sem("xin_ready")
        s_cv = sem("conv_steps")
        s_z = sem("z_ready")
        s_sz = sem("z_silu")
        s_xc = sem("xc_silu")
        s_bc = sem("bc_ready")
        s_spa = sem("softplus_act")
        s_dt = sem("dt_ready")
        s_dx = sem("dtx_ready")
        s_pc = sem("pieces_act")
        s_re = sem("pieces_pool")
        s_sk = [sem("stack0_loaded"), sem("stack1_loaded")]
        s_bdt = sem("dt_broadcast")
        s_bdx = sem("dtx_broadcast")
        s_de = sem("decay_ready")
        s_dr = sem("drive_ready")
        s_h = sem("state_ready")
        s_pr = sem("product_ready")
        s_ca = sem("carry_ready")
        s_y = sem("y_groups")
        s_ys = sem("y_skip")
        s_yg = sem("y_gated")
        s_xr = sem("xres_loaded")
        s_op = sem("out_projected")
        s_x2 = sem("x2_ready")
        s_st2 = sem("c_stats")
        s_rs2 = sem("c_rstd")
        s_xn2 = sem("c_normalized")
        s_t2 = sem("xn2_transposed")
        s_x2T = sem("xn2T_ready")
        s_lo = sem("router_full")
        s_rt = sem("routing_steps")
        s_ex = sem("router_exp")
        s_gt = sem("gates_transposed")
        s_gT = sem("gT_ready")
        s_b2 = sem("b2_full")
        s_ai = sem("b2_added")
        s_l1 = sem("hidden_full")
        s_re1 = sem("relu_ready")
        s_l2 = sem("expert_full")
        s_ad = sem("expert_added")
        s_ao = sem("acc_parts")
        s_out = sem("out_stored")
        R_STEPS = 18
        SMALL = 5
        FFN = 6
        NR = DI // NS
        EXPERTS_BEFORE_BIAS = sum(at < DVE_AT["bias"] for at in ADD_AT)

        block = ctx.enter_context(nc.Block())

        def steps(eng, step):
            step(0, None, None, 0)
            step(1, 0, None, 1)
            with eng.Fori(0, n_pairs - 1) as k:
                step(2 * k + 2, 2 * k + 1, 2 * k, 0)
                step(2 * k + 3, 2 * k + 2, 2 * k + 1, 1)
            step(None, n_chunks - 1, n_chunks - 2, 0)
            step(None, None, n_chunks - 1, 1)

        def nonneg(eng, s, value):
            if isinstance(value, int) and value <= 0:
                return
            eng.wait_ge(s, value)

        @block.sync
        def _(sp):
            sp.dma_start(cst[:, :], consts).then_inc(s_w1, 16)
            sp.dma_start(chn[:, :], chan).then_inc(s_w1, 16)
            sp.dma_start(win_c[:, :], w_in).then_inc(s_w1, 16)
            sp.dma_start(wdt_b[:, :], w_dt.partition_broadcast(P)).then_inc(s_w1, 16)
            sp.dma_start(alog[:, :], a_log).then_inc(s_w1, 16)
            sp.dma_start(w1[:, :, :], w_1.rearrange("e d h -> d e h")).then_inc(s_w2, 16)
            sp.dma_start(w2[:, :, :, :], w_2.rearrange("e (k h) d -> h e k d", h=P)).then_inc(s_w2, 16)
            sp.dma_start(wr[:, :], w_r).then_inc(s_w2, 16)
            sp.dma_start(br[:, :], b_r).then_inc(s_w2, 16)
            sp.dma_start(b1[:, :], b_1).then_inc(s_w2, 16)
            sp.dma_start(b2[:, :], b_2).then_inc(s_w2, 16)

            def load(dst, c, done):
                rows = x[bass.ds(c * TOK, TOK), :].rearrange("(t p) c -> p t c", p=P)
                sp.dma_start(dst[:, :, :], rows).then_inc(done, 16)

            def step(ca, cb, cc, par):
                if ca is not None:
                    nonneg(sp, s_bdx, DI * (ca - 1))
                    for T in range(NT):
                        for piece in range(3):
                            if piece < 2:
                                sp.wait_ge(s_pc, 8 * ca + 4 * T + 2 * piece + 2)
                            else:
                                sp.wait_ge(s_re, 8 * ca + 4 * T + 4)
                            for s in range(NS):
                                sp.dma_start(stack[32 * piece:32 * piece + 32, par, T, s, :, :],
                                             pieces[32 * s:32 * s + 32, T, piece, :, :]).then_inc(s_sk[T], 16)
                if cc is not None:
                    sp.wait_ge(s_ad, 1 + E * (cc + 1))
                    rows = out[bass.ds(cc * TOK, TOK), :].rearrange("(t p) c -> p t c", p=P)
                    sp.dma_start(rows, acc[:, :, :]).then_inc(s_out, 16)
                    sp.wait_ge(s_out, 16 * (cc + 1))
                    if not (isinstance(cc, int) and cc == n_chunks - 1):
                        load(xres, cc + 1, s_xr)
                elif cb is not None:
                    load(xres, 0, s_xr)

            steps(sp, step)

        @block.gpsimd
        def _(pool):
            def product(c, i, par):
                n = DI * c + i
                pool.wait_ge(s_h, n + 1)
                if i % NS == 0:
                    nonneg(pool, s_y, NR * c + i // NS - 1)
                if i == 0:
                    pool.wait_ge(s_bc, 2 * c + 2)
                pool.tensor_tensor(prod[:, n_mod(i), :], state[:, n_mod(i), :], bc[:, par, 1, :],
                                   ALU.mult).then_inc(s_pr, 1)

            def step(ca, cb, cc, par):
                bpar = 1 - par
                for i in range(DI):
                    if cb is not None:
                        product(cb, i, bpar)
                        if bpar == 0 and i % NS == NS - 1:
                            g = i // NS
                            r = n_mod(i - NS + 1)
                            pool.tensor_copy(carry[:, NS * g:NS * g + NS],
                                             state[:, r:r + NS, TOK - 1]).then_inc(s_ca, 1)
                        if i == POOL_AT["gate0"]:
                            gate(cb, 0, bpar)
                    if cc is not None:
                        if i == POOL_AT["gate1"]:
                            gate(cc, 1, par)
                        if i == POOL_AT["rstd2"]:
                            pool.wait_ge(s_st2, 9 * cc + 9)
                            pool.tensor_tensor(rstdc[:, :], varc[:, :], minus_half[:, :], ALU.pow).then_inc(s_rs2, 1)
                    if ca is not None:
                        if i == POOL_AT["rstd"]:
                            pool.wait_ge(s_st, 9 * ca + 9)
                            pool.tensor_tensor(rstd[:, :], var[:, :], minus_half[:, :], ALU.pow).then_inc(s_rs, 1)
                        for T in range(NT):
                            if i == POOL_AT[f"mul{T}"]:
                                pool.wait_ge(s_dt, 2 * ca + T + 1)
                                pool.tensor_tensor(val[:, 1, T, :], val[:, 0, T, :], xc[:, par, T, :],
                                                   ALU.mult).then_inc(s_dx, 1)
                            for w in range(2):
                                if i == POOL_AT[f"re{T}{w}"]:
                                    if w == 0:
                                        pool.wait_ge(s_dx, 2 * ca + T + 1)
                                    pool.wait_ge(s_pc, 8 * ca + 4 * T + w + 1)
                                    pool.tensor_tensor(val[:, w, T, :], val[:, w, T, :], pieces[:, T, 0, w, :],
                                                       ALU.subtract).then_inc(s_re, 1)
                            for w in range(2):
                                if i == POOL_AT[f"re{T}{2 + w}"]:
                                    pool.wait_ge(s_re, 8 * ca + 4 * T + w + 1)
                                    pool.wait_ge(s_pc, 8 * ca + 4 * T + 2 + w + 1)
                                    pool.tensor_tensor(pieces[:, T, 2, w, :], val[:, w, T, :], pieces[:, T, 1, w, :],
                                                       ALU.subtract).then_inc(s_re, 1)

            def gate(c, T, par):
                pool.wait_ge(s_ys, 2 * c + T + 1)
                pool.wait_ge(s_sz, 2 * c + 2)
                pool.tensor_tensor(yg[:, T, :], yg[:, T, :], sz[:, par, T, :], ALU.mult).then_inc(s_yg, 1)

            pool.wait_ge(s_sel, 1)
            steps(pool, step)

        @block.scalar
        def _(act):
            act.wait_ge(s_w1, 16 * SMALL)
            act.preload_act_table_set("natural_log_exp_and_others")
            act.activation(pos_a[:, :], alog[:, :], ACT.Exp).then_inc(s_apos, 1)

            def decays(c, i):
                n = DI * c + i
                T, q, s = channel(i)
                d = DT * T + NQ * s + q
                act.wait_ge(s_bdt, n + 1)
                nonneg(act, s_h, n - RING + 1)
                act.activation(decay[:, n_mod(i), :], ps_dt[i % 2][:, :], ACT.Exp,
                               scale=neg_a[:, d:d + 1]).then_inc(s_de, 1)

            def a_copy(dst, job, c, done):
                act.wait_ge(s_ta, 9 * c + job + 1)
                act.activation(dst, ps_a[:, :], ACT.Copy).then_inc(done, 1)

            def softplus(c, T, k):
                if k == 0:
                    act.wait_ge(s_ta, 9 * c + 7 + T + 1)
                    if T == 0:
                        nonneg(act, s_re, 8 * c)
                    act.activation(val[:, 0, T, :], ps_a[:, :], ACT.Identity,
                                   bias=chn[:, C_BDT + T:C_BDT + T + 1]).then_inc(s_spa, 1)
                else:
                    act.wait_ge(s_spa, 8 * c + 4 * T + k)
                if k == 1:
                    nonneg(act, s_dt, 2 * c + T)
                    act.activation(soft[:, :], val[:, 0, T, :], ACT.Abs).then_inc(s_spa, 1)
                if k == 2:
                    act.activation(soft[:, :], soft[:, :], ACT.Exp, scale=-1.0).then_inc(s_spa, 1)
                if k == 3:
                    act.activation(soft[:, :], soft[:, :], ACT.Ln, bias=1.0).then_inc(s_spa, 1)

            def relu(c, e, half):
                act.wait_ge(s_l1, 2 * E * c + 2 * e + half + 1)
                if e >= 2:
                    act.wait_ge(s_l2, E * c + e - 1)
                act.activation(hid[:, e % 2, half, :], ps_c[0][:, :], ACT.Relu,
                               bias=b1[:, 2 * e + half:2 * e + half + 1]).then_inc(s_re1, 1)

            def step(ca, cb, cc, par):
                if ca is not None:
                    nonneg(act, s_xn, TT * ca)
                    rows = x[bass.ds(ca * TOK, TOK), :].rearrange("(t p) c -> p t c", p=P)
                    act.dma_start(xt[:, :, :], rows).then_inc(s_x, 16)
                for i in range(DI):
                    if cb is not None and i + LOOK - 1 < DI:
                        decays(cb, i + LOOK - 1)
                    if ca is not None and i + LOOK - 1 >= DI:
                        decays(ca, i + LOOK - 1 - DI)
                    if cc is not None:
                        if i == ACT_AT["turn2"]:
                            act.wait_ge(s_t2, cc + 1)
                            act.activation(xn2T[:, :], ps_c[0][:, :], ACT.Copy).then_inc(s_x2T, 1)
                        if i == ACT_AT["expo"]:
                            act.wait_ge(s_rt, R_STEPS * cc + 12)
                            act.activation(expo[:, :, :], shifted[:, :, :], ACT.Exp).then_inc(s_ex, 1)
                        if i == ACT_AT["gates"]:
                            act.wait_ge(s_gt, cc + 1)
                            act.activation(gT[:, :], ps_a[0:E, :], ACT.Copy).then_inc(s_gT, 1)
                        for unit in range(2 * E):
                            if i == RELU_AT[unit]:
                                relu(cc, unit // 2, unit % 2)
                    if ca is not None:
                        if i == ACT_AT["xnT"]:
                            a_copy(xnT[:, :], 0, ca, s_xnT)
                        if i == ACT_AT["xin0"]:
                            act.wait_ge(s_pad, ca + 1)
                            a_copy(xin[:, 0, TAPS - 1:], 1, ca, s_xin)
                        if i == ACT_AT["xin1"]:
                            a_copy(xin[:, 1, TAPS - 1:], 2, ca, s_xin)
                        for T in range(NT):
                            if i == ACT_AT[f"z{T}"]:
                                if T == 0:
                                    nonneg(act, s_yg, 2 * (ca - 1))
                                a_copy(sz[:, par, T, :], 3 + T, ca, s_z)
                        if i == ACT_AT["silu"]:
                            for T in range(NT):
                                act.wait_ge(s_z, 2 * ca + T + 1)
                                act.activation(sz[:, par, T, :], sz[:, par, T, :], ACT.Silu).then_inc(s_sz, 1)
                            for T in range(NT):
                                act.wait_ge(s_cv, 8 * ca + 7 + T)
                                act.activation(xc[:, par, T, :], cv[:, T, :], ACT.Silu).then_inc(s_xc, 1)
                            act.preload_act_table_set("natural_log_exp_and_others")
                        if i == ACT_AT["b"]:
                            nonneg(act, s_pr, DI * (ca - 1))
                            a_copy(bc[:, par, 0, :], 5, ca, s_bc)
                        if i == ACT_AT["c"]:
                            a_copy(bc[:, par, 1, :], 6, ca, s_bc)
                        for T in range(NT):
                            for k in range(4):
                                if i == ACT_AT[f"sp{T}{k}"]:
                                    softplus(ca, T, k)
                        for T in range(NT):
                            for w in range(2):
                                if i == ACT_AT[f"pc{T}{w}"]:
                                    if w == 0:
                                        nonneg(act, s_sk[T], 16 * 12 * ca)
                                        act.wait_ge(s_dt, 2 * ca + T + 1)
                                    else:
                                        act.wait_ge(s_dx, 2 * ca + T + 1)
                                    act.activation(pieces[:, T, 0, w, :], val[:, w, T, :], ACT.Copy).then_inc(s_pc, 1)
                            for w in range(2):
                                if i == ACT_AT[f"pc{T}{2 + w}"]:
                                    act.wait_ge(s_re, 8 * ca + 4 * T + w + 1)
                                    act.activation(pieces[:, T, 1, w, :], val[:, w, T, :], ACT.Copy).then_inc(s_pc, 1)

            act.wait_ge(s_aneg, 1)
            steps(act, step)

        @block.tensor
        def _(pe):
            pe.wait_ge(s_w1, 16 * SMALL)
            pe.wait_ge(s_sel, 1)
            pe.wait_ge(s_wmix, 1)

            def bcast(c, i, w, par):
                n = DI * c + i
                T, q, s = channel(i)
                if w == 0:
                    nonneg(pe, s_de, n - 1)
                    bank, done = ps_dt[i % 2], s_bdt
                else:
                    nonneg(pe, s_dr, n - 1)
                    bank, done = ps_dx[i % 2], s_bdx
                pe.matmul(bank[:, :], sel[:, q, :], stack[:, par, T, s, w, :],
                          start=True, stop=True).then_inc(done, 1)

            def y_group(c, g):
                q = g % NQ
                pe.wait_ge(s_pr, DI * c + NS * g + NS)
                if q == 0:
                    nonneg(pe, s_ys, 2 * c + g // NQ)
                for s in range(NS):
                    mm = pe.matmul(ps_y[32 * s:32 * s + 32, :], ysel[:, q, :], prod[:, n_mod(NS * g + s), :],
                                   start=(q == 0), stop=(q == NQ - 1))
                mm.then_inc(s_y, 1)

            def project(weights, rhs):
                for j, (a, b) in enumerate(zip(weights, rhs)):
                    mm = pe.matmul(ps_a[:, :], a, b, start=(j == 0), stop=(j == len(weights) - 1))
                mm.then_inc(s_ta, 1)

            def stage_a(c, i, par):
                xcs = [xc[:, par, T, :] for T in range(NT)]
                if i == PE_AT["turn"]:
                    nonneg(pe, s_spa, 8 * c)
                    nonneg(pe, s_ai, c - 1)
                    pe.wait_ge(s_xn, TT * (c + 1))
                    for t in range(TT):
                        mm = pe.transpose(ps_a[:, t * P:(t + 1) * P], xn[:, t, :], ident)
                    mm.then_inc(s_ta, 1)
                if i == PE_AT["in0"]:
                    pe.wait_ge(s_xnT, c + 1)
                    project([win2[:, 0, :]], [xnT[:, :]])
                if i == PE_AT["in1"]:
                    pe.wait_ge(s_xin, 2 * c + 1)
                    project([win2[:, 1, :]], [xnT[:, :]])
                if i == PE_AT["in2"]:
                    pe.wait_ge(s_xin, 2 * c + 2)
                    project([win2[:, 2, :]], [xnT[:, :]])
                if i == PE_AT["in3"]:
                    pe.wait_ge(s_z, 2 * c + 1)
                    project([win2[:, 3, :]], [xnT[:, :]])
                if i == PE_AT["b"]:
                    pe.wait_ge(s_z, 2 * c + 2)
                    pe.wait_ge(s_xc, 2 * c + 2)
                    project([wbc2[:, 0, T, :] for T in range(NT)], xcs)
                if i == PE_AT["c"]:
                    pe.wait_ge(s_bc, 2 * c + 1)
                    project([wbc2[:, 1, T, :] for T in range(NT)], xcs)
                if i == PE_AT["dt0"]:
                    pe.wait_ge(s_bc, 2 * c + 2)
                    project([wdt2[:, T, 0, :] for T in range(NT)], xcs)
                if i == PE_AT["dt1"]:
                    pe.wait_ge(s_spa, 8 * c + 1)
                    project([wdt2[:, T, 1, :] for T in range(NT)], xcs)

            def hidden(c, e, half):
                if (e, half) == (0, 0):
                    pe.wait_ge(s_x2T, c + 1)
                else:
                    pe.wait_ge(s_re1, 2 * E * c + 2 * e + half)
                pe.matmul(ps_c[0][:, :], w1[:, e, half * P:(half + 1) * P], xn2T[:, :],
                          start=True, stop=True).then_inc(s_l1, 1)

            def expert_out(c, e, part):
                if part == 0:
                    pe.wait_ge(s_re1, 2 * E * c + 2 * e + 2)
                    if e == 0:
                        pe.wait_ge(s_rt, R_STEPS * c + 1)
                    else:
                        pe.wait_ge(s_ad, 1 + E * c + e)
                for t in range(2 * part, 2 * part + 2):
                    for half in range(2):
                        mm = pe.matmul(ps_c[1][:, t * P:(t + 1) * P], hid[:, e % 2, half, t * P:(t + 1) * P],
                                       w2[:, e, half, :], start=(half == 0), stop=(half == 1))
                if part == 1:
                    mm.then_inc(s_l2, 1)

            def stage_c(c, i):
                if i == PE_AT["y"]:
                    y_group(c, NR - 1)
                if i == PE_AT["out"]:
                    pe.wait_ge(s_yg, 2 * c + 2)
                    pe.wait_ge(s_ad, 1 + E * c)
                    for t in range(TT):
                        for T in range(NT):
                            mm = pe.matmul(ps_c[1][:, t * P:(t + 1) * P], yg[:, T, t * P:(t + 1) * P],
                                           wout2[:, T, :], start=(T == 0), stop=(T == NT - 1))
                    mm.then_inc(s_op, 1)
                if i == PE_AT["turn2"]:
                    pe.wait_ge(s_xn2, TT * (c + 1))
                    for t in range(TT):
                        mm = pe.transpose(ps_c[0][:, t * P:(t + 1) * P], xn2[:, t, :], ident)
                    mm.then_inc(s_t2, 1)
                if i == PE_AT["route"]:
                    pe.wait_ge(s_x2T, c + 1)
                    pe.wait_ge(s_x2, c + 1)
                    if isinstance(c, int):
                        pe.wait_ge(s_w2, 16 * FFN)
                    for t in range(TT):
                        cols = ps_c[1][:, t * E:(t + 1) * E]
                        pe.matmul(cols, xn2T[:, t * P:(t + 1) * P], wr[:, :], start=True, stop=False)
                        mm = pe.matmul(cols, ones[:, :], br[:, :], start=False, stop=True)
                    mm.then_inc(s_lo, 1)
                if i == PE_AT["gates"]:
                    pe.wait_ge(s_rt, R_STEPS * (c + 1))
                    pe.wait_ge(s_spa, a_done(c, 8, 5))
                    for t in range(TT):
                        mm = pe.matmul(ps_a[0:E, t * P:(t + 1) * P], gates[:, t, :], ident, start=True, stop=True)
                    mm.then_inc(s_gt, 1)
                if i == PE_AT["bias"]:
                    pe.wait_ge(s_gT, c + 1)
                    for t in range(TT):
                        mm = pe.matmul(ps_a[:, t * P:(t + 1) * P], gT[:, t * P:(t + 1) * P], b2[:, :],
                                       start=True, stop=True)
                    mm.then_inc(s_b2, 1)
                for unit in range(2 * E):
                    if i == HIDDEN_AT[unit]:
                        hidden(c, unit // 2, unit % 2)
                    if unit >= 2 and i == EXPERT_AT[unit - 2]:
                        expert_out(c, unit // 2 - 1, unit % 2)
                for part in range(2):
                    if i == EXPERT_AT[2 * E - 2 + part]:
                        expert_out(c, E - 1, part)

            def a_done(c, per, at):
                if isinstance(c, int) and c + 2 >= n_chunks:
                    return per * n_chunks
                return per * (c + 2) + at

            def step(ca, cb, cc, par):
                bpar = 1 - par
                for i in range(DI):
                    if cb is not None:
                        if i + LOOK == DT:
                            pe.wait_ge(s_sk[1], 16 * 12 * (cb + 1))
                        if i + LOOK < DI:
                            bcast(cb, i + LOOK, 0, bpar)
                        if i + 1 < DI:
                            bcast(cb, i + 1, 1, bpar)
                        if i >= Y_AT and (i - Y_AT) % NS == 0:
                            y_group(cb, (i - Y_AT) // NS)
                    if ca is not None and i + LOOK >= DI:
                        if i + LOOK == DI:
                            pe.wait_ge(s_sk[0], 16 * 12 * (ca + 1))
                        bcast(ca, i + LOOK - DI, 0, par)
                        if i == DI - 1:
                            bcast(ca, 0, 1, par)
                    if cc is not None:
                        stage_c(cc, i)
                    if ca is not None:
                        stage_a(ca, i, par)

            win2 = win[:, :, :].rearrange("p (m e) h -> p m (e h)", m=4)
            wbc2 = wbc[:, :, :, :, :].rearrange("p b t h n -> p b t (h n)")
            wdt2 = wdt[:, :, :, :, :].rearrange("p k t d h -> p k t (d h)")
            wout2 = wout[:, :, :, :].rearrange("p t h i -> p t (h i)")
            steps(pe, step)

        @block.vector
        def _(dve):
            dve.wait_ge(s_w1, 16 * SMALL)
            dve.memset(ones[:, :], 1.0)
            dve.memset(minus_half[:, :], -0.5)
            dve.tensor_copy(sel[:, :, :], cst[0:96, K_SEL:K_SEL + NQ * P].rearrange("p (q m) -> p q m", q=NQ)
                            ).then_inc(s_sel, 1)
            dve.tensor_tensor(win[:, :, :], win_c[:, :].unsqueeze(2).to_broadcast([P, 4 * DT, H]),
                              head_of_in.unsqueeze(1).to_broadcast([P, 4 * DT, H]), ALU.mult)
            for T in range(NT):
                for b in range(2):
                    dve.tensor_tensor(wbc[:, b, T, :, :],
                                      wxp[:, T, 1 + N * b:1 + N * b + N].unsqueeze(1).to_broadcast([P, H, N]),
                                      head_of_ch.unsqueeze(2).to_broadcast([P, H, N]), ALU.mult)
                for T2 in range(NT):
                    dve.scalar_tensor_tensor(
                        out=wdt[:, T, T2, :, :],
                        in0=wdt_b[:, T2 * DT * H:(T2 + 1) * DT * H].rearrange("p (d h) -> p d h", h=H),
                        scalar=wxp[:, T, 0:1], in1=head_of_ch.unsqueeze(1).to_broadcast([P, DT, H]),
                        op0=ALU.mult, op1=ALU.mult)
                last = dve.tensor_tensor(
                    wout[:, T, :, :],
                    chn[:, C_WO + T * DH:C_WO + (T + 1) * DH].unsqueeze(1).to_broadcast([P, H, DH]),
                    head_of_ch.unsqueeze(2).to_broadcast([P, H, DH]), ALU.mult)
            last.then_inc(s_wmix, 1)
            dve.wait_ge(s_apos, 1)
            dve.tensor_scalar(neg_a[:, :], pos_a[:, :], -1.0, None, ALU.mult).then_inc(s_aneg, 1)
            dve.wait_ge(s_aneg, 1)
            dve.memset(both[:, :, :], 0.0).then_inc(s_ad, 1)
            dve.memset(inv[:, :], 0.0).then_inc(s_ai, 1)

            def drives(c, i, par):
                n = DI * c + i
                dve.wait_ge(s_bdx, n + 1)
                nonneg(dve, s_h, n - 3)
                dve.tensor_tensor(drive[:, i % 4, :], ps_dx[i % 2][:, :], bc[:, par, 0, :],
                                  ALU.mult).then_inc(s_dr, 1)

            def scan(c, i, par):
                n = DI * c + i
                dve.wait_ge(s_de, n + 1)
                dve.wait_ge(s_dr, n + 1)
                if i % NS == 0 and (i >= RING) == (par == 0):
                    nonneg(dve, s_pr, n - RING + NS + 1)
                else:
                    nonneg(dve, s_pr, n - RING + 1)
                initial = 0.0
                if par == 1:
                    if i % NS == 0:
                        dve.wait_ge(s_ca, carries(c, i))
                    initial = carry[:, i:i + 1]
                dve.tensor_tensor_scan(state[:, n_mod(i), :], decay[:, n_mod(i), :], drive[:, i % 4, :],
                                       initial, ALU.mult, ALU.add).then_inc(s_h, 1)

            def carries(c, i):
                return half(c, NR) + i // NS + 1

            def half(c, per):
                if isinstance(c, int):
                    return (c // 2) * per
                return (c - 1) * (per // 2)

            def stats(src, st, m, v, done, c, k):
                if k == 0:
                    for t in range(TT):
                        dve.bn_stats(st[:, t, :], src[:, t, :]).then_inc(done, 1)
                if k == 1:
                    for t in range(TT):
                        dve.bn_aggr(m[:, t, :], st[:, t, :]).then_inc(done, 1)
                if k == 2:
                    dve.wait_ge(done, 9 * c + 2 * TT)
                    dve.tensor_scalar(v[:, :], m[:, :, 1], EPS, None, ALU.add).then_inc(done, 1)

            def normalize(src, m, r, dst, done):
                for t in range(TT):
                    dve.tensor_scalar(dst[:, t, :], src[:, t, :], m[:, t, 0:1], r[:, t:t + 1],
                                      ALU.subtract, ALU.mult).then_inc(done, 1)

            def conv(c, k):
                for T in range(NT):
                    taps = chn[:, C_CW + TAPS * T + k:C_CW + TAPS * T + k + 1]
                    src = xin[:, T, k:k + TOK]
                    if k == 0:
                        dve.wait_ge(s_xin, 2 * c + T + 1)
                        if T == 0:
                            nonneg(dve, s_xc, 2 * c)
                        dve.tensor_scalar(cv[:, T, :], src, taps, chn[:, C_CB + T:C_CB + T + 1],
                                          ALU.mult, ALU.add).then_inc(s_cv, 1)
                    else:
                        dve.wait_ge(s_cv, 8 * c + 2 * k + T - 1)
                        dve.scalar_tensor_tensor(out=cv[:, T, :], in0=src, scalar=taps, in1=cv[:, T, :],
                                                 op0=ALU.mult, op1=ALU.add).then_inc(s_cv, 1)

            def softplus(c, T):
                dve.wait_ge(s_spa, 8 * c + 4 * T + 4)
                dve.scalar_tensor_tensor(out=val[:, 0, T, :], in0=val[:, 0, T, :], scalar=0.0, in1=soft[:, :],
                                         op0=ALU.max, op1=ALU.add).then_inc(s_dt, 1)

            def skip(c, T, par):
                dve.wait_ge(s_y, NR * c + NQ * (T + 1))
                if T == 0:
                    nonneg(dve, s_op, c)
                dve.scalar_tensor_tensor(out=yg[:, T, :], in0=xc[:, par, T, :],
                                         scalar=chn[:, C_DP + T:C_DP + T + 1], in1=ps_y[:, :],
                                         op0=ALU.mult, op1=ALU.add).then_inc(s_ys, 1)

            def over_e(ap):
                return ap.unsqueeze(2).to_broadcast([P, TT, E])

            def routing(c, k):
                base = R_STEPS * c
                if k > 0:
                    dve.wait_ge(s_rt, base + k)
                if k == 0:
                    dve.wait_ge(s_lo, c + 1)
                    op = dve.tensor_copy(lg[:, :, :], ps_c[1][:, 0:TT * E].rearrange("p (t e) -> p t e", t=TT))
                elif k == 1:
                    op = dve.tensor_reduce(top[:, 0, :], lg[:, :, :], AX_X, ALU.max)
                elif k == 2:
                    op = dve.tensor_tensor(eq[:, 0, :, :], lg[:, :, :], over_e(top[:, 0, :]), ALU.is_equal)
                elif k == 3:
                    op = dve.tensor_tensor(eq[:, 0, :, :], eq[:, 0, :, :], order, ALU.mult)
                elif k == 4:
                    op = dve.tensor_reduce(first[:, 0, :], eq[:, 0, :, :], AX_X, ALU.max)
                elif k == 5:
                    op = dve.tensor_tensor(pick[:, 0, :, :], eq[:, 0, :, :], over_e(first[:, 0, :]), ALU.is_equal)
                elif k == 6:
                    op = dve.scalar_tensor_tensor(out=lg2[:, :, :], in0=pick[:, 0, :, :], scalar=-BIG,
                                                  in1=lg[:, :, :], op0=ALU.mult, op1=ALU.add)
                elif k == 7:
                    op = dve.tensor_reduce(top[:, 1, :], lg2[:, :, :], AX_X, ALU.max)
                elif k == 8:
                    op = dve.tensor_tensor(eq[:, 1, :, :], lg2[:, :, :], over_e(top[:, 1, :]), ALU.is_equal)
                elif k == 9:
                    op = dve.tensor_tensor(eq[:, 1, :, :], eq[:, 1, :, :], order, ALU.mult)
                elif k == 10:
                    op = dve.tensor_reduce(first[:, 1, :], eq[:, 1, :, :], AX_X, ALU.max)
                elif k == 11:
                    op = dve.tensor_tensor(shifted[:, :, :], lg[:, :, :], over_e(top[:, 0, :]), ALU.subtract)
                elif k == 12:
                    op = dve.tensor_tensor(pick[:, 1, :, :], eq[:, 1, :, :], over_e(first[:, 1, :]), ALU.is_equal)
                elif k == 13:
                    op = dve.tensor_tensor(both[:, :, :], pick[:, 0, :, :], pick[:, 1, :, :], ALU.add)
                elif k == 14:
                    dve.wait_ge(s_ex, c + 1)
                    op = dve.tensor_tensor(masked[:, :, :], expo[:, :, :], both[:, :, :], ALU.mult)
                elif k == 15:
                    op = dve.tensor_reduce(total[:, :], masked[:, :, :], AX_X, ALU.add)
                elif k == 16:
                    op = dve.reciprocal(inv[:, :], total[:, :])
                elif k == 17:
                    op = dve.tensor_tensor(gates[:, :, :], masked[:, :, :], over_e(inv[:, :]), ALU.mult)
                op.then_inc(s_rt, 1)

            def add_expert(c, e):
                dve.wait_ge(s_l2, E * c + e + 1)
                if e == 0:
                    dve.wait_ge(s_rt, R_STEPS * (c + 1))
                    before = x2
                else:
                    dve.wait_ge(s_ad, 1 + E * c + e)
                    before = acc
                if e == EXPERTS_BEFORE_BIAS:
                    dve.wait_ge(s_ai, c + 2)
                for t in range(TT):
                    op = dve.scalar_tensor_tensor(out=acc[:, t, :], in0=ps_c[1][:, t * P:(t + 1) * P],
                                                  scalar=gates[:, t, e:e + 1], in1=before[:, t, :],
                                                  op0=ALU.mult, op1=ALU.add)
                op.then_inc(s_ad, 1)

            def add_bias(c):
                dve.wait_ge(s_b2, c + 1)
                dve.wait_ge(s_ad, 1 + E * c + EXPERTS_BEFORE_BIAS)
                dve.tensor_tensor(acc[:, :, :], ps_a[:, :].rearrange("p (t d) -> p t d", t=TT),
                                  acc[:, :, :], ALU.add).then_inc(s_ai, 1)

            def stage_a(c, j, par):
                if j == DVE_AT["stat0"]:
                    dve.wait_ge(s_x, 16 * (c + 1))
                    stats(xt, st6, mv, var, s_st, c, 0)
                if j == DVE_AT["stat1"]:
                    stats(xt, st6, mv, var, s_st, c, 1)
                if j == DVE_AT["stat2"]:
                    stats(xt, st6, mv, var, s_st, c, 2)
                if j == DVE_AT["norm"]:
                    dve.wait_ge(s_rs, c + 1)
                    nonneg(dve, s_ta, 9 * (c - 1) + 1)
                    normalize(xt, mv, rstd, xn, s_xn)
                if j == DVE_AT["pad"]:
                    nonneg(dve, s_cv, 8 * c)
                    if par == 0:
                        dve.memset(xin[:, :, 0:TAPS - 1], 0.0).then_inc(s_pad, 1)
                    else:
                        dve.tensor_copy(xin[:, :, 0:TAPS - 1], xin[:, :, TOK:TOK + TAPS - 1]).then_inc(s_pad, 1)
                for k in range(TAPS):
                    if j == DVE_AT[f"conv{k}"]:
                        if k == 0:
                            dve.wait_ge(s_pad, c + 1)
                        conv(c, k)
                for T in range(NT):
                    if j == DVE_AT[f"dt{T}"]:
                        softplus(c, T)

            def stage_c(c, j, par):
                if j == DVE_AT["skip1"]:
                    skip(c, 1, par)
                if j == DVE_AT["x2"]:
                    dve.wait_ge(s_op, c + 1)
                    dve.wait_ge(s_xr, 16 * (c + 1))
                    dve.tensor_tensor(x2[:, :, :], ps_c[1][:, :].rearrange("p (t d) -> p t d", t=TT),
                                      xres[:, :, :], ALU.add).then_inc(s_x2, 1)
                if j == DVE_AT["cstat0"]:
                    dve.wait_ge(s_x2, c + 1)
                    stats(x2, st6c, mvc, varc, s_st2, c, 0)
                if j == DVE_AT["cstat1"]:
                    stats(x2, st6c, mvc, varc, s_st2, c, 1)
                if j == DVE_AT["cstat2"]:
                    stats(x2, st6c, mvc, varc, s_st2, c, 2)
                if j == DVE_AT["norm2"]:
                    dve.wait_ge(s_rs2, c + 1)
                    normalize(x2, mvc, rstdc, xn2, s_xn2)
                for k in range(R_STEPS):
                    if j == ROUTE_AT[k]:
                        routing(c, k)
                if j == DVE_AT["bias"]:
                    add_bias(c)
                for e in range(E):
                    if j == ADD_AT[e]:
                        add_expert(c, e)

            def step(ca, cb, cc, par):
                bpar = 1 - par
                for j in range(2 * DI):
                    i = j // 2
                    if ca is not None and j == DVE_AT["stat1"]:
                        dve.wait_ge(s_st, 9 * ca + TT)
                    if cc is not None and j == DVE_AT["cstat1"]:
                        dve.wait_ge(s_st2, 9 * cc + TT)
                    if cb is not None:
                        if j % 2 == 0 and i + 1 < DI:
                            drives(cb, i + 1, bpar)
                        if j % 2 == 1:
                            scan(cb, i, bpar)
                        if j == DVE_AT["skip0"]:
                            skip(cb, 0, bpar)
                    if ca is not None and j == 2 * DI - 2:
                        dve.wait_ge(s_bc, 2 * ca + 1)
                        drives(ca, 0, par)
                    if cc is not None:
                        stage_c(cc, j, par)
                    if ca is not None:
                        stage_a(ca, j, par)

            steps(dve, step)


def n_mod(i):
    return i % RING


def kernel(L0_attn_x, L0_attn_W_in, L0_attn_conv_w, L0_attn_conv_b, L0_attn_W_xp, L0_attn_W_dt,
           L0_attn_b_dt, L0_attn_A_log, L0_attn_Dp, L0_attn_W_out, L0_ffn_Wr, L0_ffn_br, L0_ffn_W1,
           L0_ffn_b1, L0_ffn_W2, L0_ffn_b2):
    import numpy as np
    import concourse.bacc as bacc
    from concourse.bass_utils import run_bass_kernel_spmd

    c = np.zeros((P, K_END), np.float32)
    rows = np.arange(P)
    c[rows, K_ID + rows] = 1
    for q in range(NQ):
        for h in range(H):
            for piece in range(3):
                c[32 * piece + 8 * q + h, K_SEL + P * q + N * h:K_SEL + P * q + N * h + N] = 1
            c[N * h:N * h + N, K_YSEL + 32 * q + 8 * q + h] = 1
    c[rows, K_HM1 + rows // DH] = 1
    c[rows, K_HM2 + rows % H] = 1
    c[:, K_ORD:K_END] = np.tile(np.arange(E, 0, -1), TT)

    def by_channel(a):
        a = np.asarray(a).reshape((H, NT, DT) + a.shape[2:])
        a = np.moveaxis(a, (2, 0, 1), (0, 1, 2))
        return np.ascontiguousarray(a).reshape(P, -1)

    chan = np.concatenate([by_channel(a) for a in (L0_attn_conv_w, L0_attn_conv_b, L0_attn_W_xp,
                                                   L0_attn_b_dt, L0_attn_Dp, L0_attn_W_out)], axis=1)
    arrays = {
        "x_in": np.ascontiguousarray(L0_attn_x).reshape(-1, P),
        "consts_in": c,
        "chan_in": chan,
        "w_in_in": np.ascontiguousarray(L0_attn_W_in).reshape(P, 4 * DT),
        "w_dt_in": np.ascontiguousarray(np.transpose(np.asarray(L0_attn_W_dt)[:, 0, :], (1, 0))).reshape(-1),
        "a_log_in": np.ascontiguousarray(np.transpose(np.asarray(L0_attn_A_log), (0, 2, 1))).reshape(P, DI),
        "w_r_in": np.ascontiguousarray(L0_ffn_Wr),
        "b_r_in": np.ascontiguousarray(L0_ffn_br).reshape(1, E),
        "w_1_in": np.ascontiguousarray(L0_ffn_W1),
        "b_1_in": np.ascontiguousarray(np.transpose(np.asarray(L0_ffn_b1).reshape(2 * E, P), (1, 0))),
        "w_2_in": np.ascontiguousarray(L0_ffn_W2),
        "b_2_in": np.ascontiguousarray(L0_ffn_b2),
    }
    nc = bacc.Bacc("TRN2", target_bir_lowering=False, num_devices=1)
    args = [nc.dram_tensor(name, a.shape, mybir.dt.from_np(a.dtype), kind="ExternalInput").ap()
            for name, a in arrays.items()]
    shape = tuple(L0_attn_x.shape)
    out = nc.dram_tensor("block_out", (shape[0] * shape[1], P), F32, kind="ExternalOutput").ap()
    build(nc, *args, out)
    r = run_bass_kernel_spmd(nc, [arrays], core_ids=[0])
    return np.asarray(r.results[0]["block_out"]).reshape(shape)
```

```python
from contextlib import ExitStack

import concourse.bass as bass
from concourse import mybir

F32 = mybir.dt.float32
BF16 = mybir.dt.bfloat16
ALU = mybir.AluOpType
ACT = mybir.ActivationFunctionType
AX_X = mybir.AxisListType.X

P = 128
H = 8
DH = P // H
NT, NS, NQ = 2, 4, 4
DI = NT * NS * NQ
DT = NS * NQ
N = 16
E = 8
HID = 256
TOK = 512
SEQ = 1024
TT = TOK // P
TAPS = 4
EPS = 1e-5
XP = 1 + 2 * N
RING = 8
LOOK = 3
BIG = 3.0e38
PE_AT = dict(turn=4, in0=5, in1=6, in2=7, in3=9, b=15, c=17, dt0=11, dt1=13, y=3, out=5, turn2=8,
             route=10, gates=19, bias=25)
ACT_AT = dict(xnT=4, xin0=5, xin1=6, z0=8, z1=10, silu=10, b=16, c=19, sp00=11, sp01=12, sp02=12,
              sp03=12, sp10=14, sp11=15, sp12=17, sp13=18, pc00=14, pc01=16, pc02=18, pc03=21,
              pc10=25, pc11=27, pc12=29, pc13=29, turn2=8, expo=16, gates=21, norm=4, norm2=8)
DVE_AT = dict(stat0=1, stat1=3, stat2=3, pad=4, conv0=14, conv1=17, conv2=17, dt0=27, dt1=43,
              skip0=38, skip1=5, x2=9, cstat0=9, cstat1=10, cstat2=10, bias=51)
POOL_AT = dict(rstd=0, mul0=13, mul1=23, re00=14, re01=18, re02=19, re03=22, re10=23, re11=25,
               re12=27, re13=31, gate0=31, gate1=1, rstd2=4)
ROUTE_AT = [20, 21, 22, 23, 24, 25, 26, 27, 28, 28, 29, 30, 30, 32, 34, 35, 36, 37]
HIDDEN_AT = [9, 10, 12, 16, 18, 20, 20, 23, 25, 27, 28, 29, 30, 32, 34, 35]
RELU_AT = [9, 11, 14, 18, 20, 20, 21, 24, 26, 27, 28, 29, 31, 32, 33, 35]
EXPERT_AT = [12, 16, 20, 20, 23, 23, 26, 27, 29, 29, 32, 32, 34, 34, 36, 36]
ADD_AT = [37, 41, 49, 54, 59, 65, 68, 70]
Y_AT = 6

K_ID, K_SEL, K_YSEL = 0, 128, 128 + NQ * P
K_HM1 = K_YSEL + NQ * 32
K_HM2 = K_HM1 + H
K_ORD = K_HM2 + H
K_END = K_ORD + TT * E
C_CW, C_CB = 0, NT * TAPS
C_XP = C_CB + NT
C_BDT = C_XP + NT * XP
C_DP = C_BDT + NT
C_WO = C_DP + NT
C_END = C_WO + NT * DH


def channel(i):
    return i // DT, i % DT // NS, i % NS


def build(nc, x, consts, chan, w_in, w_dt, a_log, w_r, b_r, w_1, b_1, w_2, b_2, out):
    n_chunks = x.shape[0] // TOK
    n_pairs = n_chunks // 2
    ctx = ExitStack()
    with ctx:
        def sb(name, shape, dt=F32):
            return ctx.enter_context(nc.sbuf_tensor(name, shape, dt))

        def sem(name):
            return ctx.enter_context(nc.semaphore(name))

        cst = sb("cst", [P, K_END])
        chn = sb("chn", [P, C_END])
        win_c = sb("win_c", [P, 4 * DT])
        wdt_b = sb("wdt_b", [P, NT * DT * H])
        alog = sb("alog", [P, DI])
        neg_a = sb("neg_a", [P, DI])
        pos_a = sb("pos_a", [P, DI])
        wr = sb("wr", [P, E])
        br = sb("br", [1, TT * E])
        w1 = sb("w1", [P, E, HID])
        b1 = sb("b1", [P, E * 2])
        w2 = sb("w2", [P, E, 2, P])
        b2 = sb("b2", [E, P])
        sel = sb("sel", [96, NQ, P], BF16)
        win = sb("win", [P, 4 * DT, H])
        wbc = sb("wbc", [P, 2, NT, H, N])
        wdt = sb("wdt", [P, NT, NT, DT, H])
        wout = sb("wout", [P, NT, H, DH])
        ones = sb("ones", [1, P])
        minus_half = sb("minus_half", [P, TT])
        xt = sb("xt", [P, TT, P])
        st6 = sb("st6", [P, TT, 6])
        mv = sb("mv", [P, TT, 2])
        rstd = sb("rstd", [P, TT])
        neg_m = sb("neg_m", [P, TT])
        shift = sb("shift", [P, TT])
        var = sb("var", [P, TT])
        xn = sb("xn", [P, TT, P])
        xnT = sb("xnT", [P, TOK])
        xin = sb("xin", [P, NT, TOK + TAPS - 1])
        cv = sb("cv", [P, NT, TOK])
        xc = sb("xc", [P, 2, NT, TOK])
        sz = sb("sz", [P, 2, NT, TOK])
        bc = sb("bc", [P, 2, 2, TOK])
        soft = sb("soft", [P, TOK])
        val = sb("val", [P, 2, NT, TOK])
        pieces = sb("pieces", [P, NT, 3, 2, TOK], BF16)
        stack = sb("stack", [96, 2, NT, NS, 2, TOK], BF16)
        decay = sb("decay", [P, RING, TOK])
        drive = sb("drive", [P, 4, TOK])
        state = sb("state", [P, RING, TOK])
        prod = sb("prod", [P, RING, TOK])
        carry = sb("carry", [P, DI])
        yg = sb("yg", [P, NT, TOK])
        xres = sb("xres", [P, TT, P])
        x2 = sb("x2", [P, TT, P])
        st6c = sb("st6c", [P, TT, 6])
        mvc = sb("mvc", [P, TT, 2])
        varc = sb("varc", [P, TT])
        rstdc = sb("rstdc", [P, TT])
        neg_mc = sb("neg_mc", [P, TT])
        shiftc = sb("shiftc", [P, TT])
        xn2 = sb("xn2", [P, TT, P])
        xn2T = sb("xn2T", [P, TOK])
        lg = sb("lg", [P, TT, E])
        lg2 = sb("lg2", [P, TT, E])
        top = sb("top", [P, 2, TT])
        first = sb("first", [P, 2, TT])
        eq = sb("eq", [P, 2, TT, E])
        pick = sb("pick", [P, 2, TT, E])
        both = sb("both", [P, TT, E])
        shifted = sb("shifted", [P, TT, E])
        expo = sb("expo", [P, TT, E])
        masked = sb("masked", [P, TT, E])
        total = sb("total", [P, TT])
        inv = sb("inv", [P, TT])
        gates = sb("gates", [P, TT, E])
        gT = sb("gT", [E, TOK])
        hid = sb("hid", [P, 2, 2, TOK])
        acc = sb("acc", [P, TT, P])

        ps_dt = [ctx.enter_context(nc.psum_tensor(f"ps_dt{i}", [P, TOK], F32)) for i in range(2)]
        ps_dx = [ctx.enter_context(nc.psum_tensor(f"ps_dx{i}", [P, TOK], F32)) for i in range(2)]
        ps_y = ctx.enter_context(nc.psum_tensor("ps_y", [P, TOK], F32))
        ps_a = ctx.enter_context(nc.psum_tensor("ps_a", [P, TOK], F32))
        ps_c = [ctx.enter_context(nc.psum_tensor(f"ps_c{i}", [P, TOK], F32)) for i in range(2)]

        ident = cst[:, K_ID:K_ID + P]
        ysel = cst[:, K_YSEL:K_YSEL + NQ * 32].rearrange("p (q m) -> p q m", q=NQ)
        head_of_in = cst[:, K_HM1:K_HM1 + H]
        head_of_ch = cst[:, K_HM2:K_HM2 + H]
        order = cst[:, K_ORD:K_ORD + TT * E].rearrange("p (t e) -> p t e", t=TT)
        wxp = chn[:, C_XP:C_XP + NT * XP].rearrange("p (t e) -> p t e", t=NT)

        s_w1 = sem("weights_small")
        s_w2 = sem("weights_ffn")
        s_sel = sem("sel_ready")
        s_wmix = sem("mixer_weights")
        s_apos = sem("a_positive")
        s_aneg = sem("a_ready")
        s_x = sem("x_loaded")
        s_st = sem("a_stats")
        s_rs = sem("a_rstd")
        s_xn = sem("a_normalized")
        s_ta = sem("a_psum_full")
        s_xnT = sem("xnT_ready")
        s_pad = sem("pad_ready")
        s_xin = sem("xin_ready")
        s_cva = sem("conv_last_tap")
        s_cv = sem("conv_steps")
        s_z = sem("z_ready")
        s_sz = sem("z_silu")
        s_xc = sem("xc_silu")
        s_bc = sem("bc_ready")
        s_spa = sem("softplus_act")
        s_dt = sem("dt_ready")
        s_dx = sem("dtx_ready")
        s_pc = sem("pieces_act")
        s_re = sem("pieces_pool")
        s_sk = [sem("stack0_loaded"), sem("stack1_loaded")]
        s_bdt = sem("dt_broadcast")
        s_bdx = sem("dtx_broadcast")
        s_de = sem("decay_ready")
        s_dr = sem("drive_ready")
        s_h = sem("state_ready")
        s_pr = sem("product_ready")
        s_ca = sem("carry_ready")
        s_y = sem("y_groups")
        s_ys = sem("y_skip")
        s_yg = sem("y_gated")
        s_xr = sem("xres_loaded")
        s_op = sem("out_projected")
        s_x2 = sem("x2_ready")
        s_st2 = sem("c_stats")
        s_rs2 = sem("c_rstd")
        s_xn2 = sem("c_normalized")
        s_t2 = sem("xn2_transposed")
        s_x2T = sem("xn2T_ready")
        s_lo = sem("router_full")
        s_rt = sem("routing_steps")
        s_ex = sem("router_exp")
        s_gt = sem("gates_transposed")
        s_gT = sem("gT_ready")
        s_b2 = sem("b2_full")
        s_ai = sem("b2_added")
        s_l1 = sem("hidden_full")
        s_re1 = sem("relu_ready")
        s_l2 = sem("expert_full")
        s_ad = sem("expert_added")
        s_ao = sem("acc_parts")
        s_out = sem("out_stored")
        R_STEPS = 18
        SMALL = 5
        FFN = 6
        NR = DI // NS
        EXPERTS_BEFORE_BIAS = sum(at < DVE_AT["bias"] for at in ADD_AT)

        block = ctx.enter_context(nc.Block())

        def steps(eng, step):
            step(0, None, None, None, 0)
            step(1, 0, None, None, 1)
            step(2, 1, 0, None, 0)
            with eng.Fori(0, n_pairs - 2) as k:
                step(2 * k + 3, 2 * k + 2, 2 * k + 1, 2 * k, 1)
                step(2 * k + 4, 2 * k + 3, 2 * k + 2, 2 * k + 1, 0)
            step(n_chunks - 1, n_chunks - 2, n_chunks - 3, n_chunks - 4, 1)
            step(None, n_chunks - 1, n_chunks - 2, n_chunks - 3, 0)
            step(None, None, n_chunks - 1, n_chunks - 2, 1)
            step(None, None, None, n_chunks - 1, 0)

        def nonneg(eng, s, value):
            if isinstance(value, int) and value <= 0:
                return
            eng.wait_ge(s, value)

        @block.sync
        def _(sp):
            sp.dma_start(xt[:, :, :], x[0:TOK, :].rearrange("(t p) c -> p t c", p=P)).then_inc(s_x, 16)
            sp.dma_start(cst[:, :], consts).then_inc(s_w1, 16)
            sp.dma_start(chn[:, :], chan).then_inc(s_w1, 16)
            sp.dma_start(win_c[:, :], w_in).then_inc(s_w1, 16)
            sp.dma_start(wdt_b[:, :], w_dt.partition_broadcast(P)).then_inc(s_w1, 16)
            sp.dma_start(alog[:, :], a_log).then_inc(s_w1, 16)
            sp.dma_start(w1[:, :, :], w_1.rearrange("e d h -> d e h")).then_inc(s_w2, 16)
            sp.dma_start(w2[:, :, :, :], w_2.rearrange("e (k h) d -> h e k d", h=P)).then_inc(s_w2, 16)
            sp.dma_start(wr[:, :], w_r).then_inc(s_w2, 16)
            sp.dma_start(br[:, :], b_r).then_inc(s_w2, 16)
            sp.dma_start(b1[:, :], b_1).then_inc(s_w2, 16)
            sp.dma_start(b2[:, :], b_2).then_inc(s_w2, 16)

            def load(dst, c, done):
                rows = x[bass.ds(c * TOK, TOK), :].rearrange("(t p) c -> p t c", p=P)
                sp.dma_start(dst[:, :, :], rows).then_inc(done, 16)

            def step(ca, cb, cc, cd, par):
                if cd is not None:
                    sp.wait_ge(s_ad, 1 + E * (cd + 1))
                    rows = out[bass.ds(cd * TOK, TOK), :].rearrange("(t p) c -> p t c", p=P)
                    sp.dma_start(rows, acc[:, :, :]).then_inc(s_out, 16)
                if cc is not None:
                    if not (isinstance(cc, int) and cc == n_chunks - 1):
                        sp.wait_ge(s_x2, cc + 1)
                        load(xres, cc + 1, s_xr)
                elif cb is not None:
                    load(xres, 0, s_xr)
                if ca is not None:
                    nonneg(sp, s_bdx, DI * (ca - 1))
                    for T in range(NT):
                        for piece in range(3):
                            if piece < 2:
                                sp.wait_ge(s_pc, 8 * ca + 4 * T + 2 * piece + 2)
                            else:
                                sp.wait_ge(s_re, 8 * ca + 4 * T + 4)
                            for s in range(NS):
                                sp.dma_start(stack[32 * piece:32 * piece + 32, par, T, s, :, :],
                                             pieces[32 * s:32 * s + 32, T, piece, :, :]).then_inc(s_sk[T], 16)
                if ca is None and cb is None and cc is None:
                    sp.wait_ge(s_out, 16 * n_chunks)

            steps(sp, step)

        @block.gpsimd
        def _(pool):
            def product(c, i, par):
                n = DI * c + i
                pool.wait_ge(s_h, n + 1)
                if i % NS == 0:
                    nonneg(pool, s_y, NR * c + i // NS - 1)
                if i == 0:
                    pool.wait_ge(s_bc, 2 * c + 2)
                pool.tensor_tensor(prod[:, n_mod(i), :], state[:, n_mod(i), :], bc[:, par, 1, :],
                                   ALU.mult).then_inc(s_pr, 1)

            def step(ca, cb, cc, cd, par):
                bpar = 1 - par
                for i in range(DI):
                    if cb is not None:
                        product(cb, i, bpar)
                        if bpar == 0 and i % NS == NS - 1:
                            g = i // NS
                            r = n_mod(i - NS + 1)
                            pool.tensor_copy(carry[:, NS * g:NS * g + NS],
                                             state[:, r:r + NS, TOK - 1]).then_inc(s_ca, 1)
                        if i == POOL_AT["gate0"]:
                            gate(cb, 0, bpar)
                    if cc is not None:
                        if i == POOL_AT["gate1"]:
                            gate(cc, 1, par)
                        if i == POOL_AT["rstd2"]:
                            pool.wait_ge(s_st2, 10 * cc + 10)
                            inverse_std(varc, neg_mc, rstdc, shiftc, s_rs2, cc)
                    if ca is not None:
                        if i == POOL_AT["rstd"]:
                            pool.wait_ge(s_st, 10 * ca + 10)
                            inverse_std(var, neg_m, rstd, shift, s_rs, ca)
                        for T in range(NT):
                            if i == POOL_AT[f"mul{T}"]:
                                pool.wait_ge(s_dt, 2 * ca + T + 1)
                                pool.tensor_tensor(val[:, 1, T, :], val[:, 0, T, :], xc[:, par, T, :],
                                                   ALU.mult).then_inc(s_dx, 1)
                            for w in range(2):
                                if i == POOL_AT[f"re{T}{w}"]:
                                    if w == 0:
                                        pool.wait_ge(s_dx, 2 * ca + T + 1)
                                    pool.wait_ge(s_pc, 8 * ca + 4 * T + w + 1)
                                    pool.tensor_tensor(val[:, w, T, :], val[:, w, T, :], pieces[:, T, 0, w, :],
                                                       ALU.subtract).then_inc(s_re, 1)
                            for w in range(2):
                                if i == POOL_AT[f"re{T}{2 + w}"]:
                                    pool.wait_ge(s_re, 8 * ca + 4 * T + w + 1)
                                    pool.wait_ge(s_pc, 8 * ca + 4 * T + 2 + w + 1)
                                    pool.tensor_tensor(pieces[:, T, 2, w, :], val[:, w, T, :], pieces[:, T, 1, w, :],
                                                       ALU.subtract).then_inc(s_re, 1)

            def inverse_std(v, nm, r, sh, done, c):
                pool.tensor_tensor(r[:, :], v[:, :], minus_half[:, :], ALU.pow).then_inc(done, 1)
                pool.wait_ge(done, 2 * c + 1)
                pool.tensor_tensor(sh[:, :], nm[:, :], r[:, :], ALU.mult).then_inc(done, 1)

            def gate(c, T, par):
                pool.wait_ge(s_ys, 2 * c + T + 1)
                pool.wait_ge(s_sz, 2 * c + 2)
                pool.tensor_tensor(yg[:, T, :], yg[:, T, :], sz[:, par, T, :], ALU.mult).then_inc(s_yg, 1)

            pool.wait_ge(s_sel, 1)
            steps(pool, step)

        @block.scalar
        def _(act):
            act.wait_ge(s_w1, 16 * SMALL)
            act.preload_act_table_set("natural_log_exp_and_others")
            act.activation(pos_a[:, :], alog[:, :], ACT.Exp).then_inc(s_apos, 1)

            def decays(c, i):
                n = DI * c + i
                T, q, s = channel(i)
                d = DT * T + NQ * s + q
                act.wait_ge(s_bdt, n + 1)
                nonneg(act, s_h, n - RING + 1)
                act.activation(decay[:, n_mod(i), :], ps_dt[i % 2][:, :], ACT.Exp,
                               scale=neg_a[:, d:d + 1]).then_inc(s_de, 1)

            def a_copy(dst, job, c, done):
                act.wait_ge(s_ta, 9 * c + job + 1)
                act.activation(dst, ps_a[:, :], ACT.Copy).then_inc(done, 1)

            def normalize(src, r, sh, dst, done):
                for t in range(TT):
                    act.activation(dst[:, t, :], src[:, t, :], ACT.Identity, scale=r[:, t:t + 1],
                                   bias=sh[:, t:t + 1]).then_inc(done, 1)

            def last_tap(c, T):
                if T == 0:
                    nonneg(act, s_xc, 2 * c)
                k = C_CW + TAPS * T + TAPS - 1
                act.activation(cv[:, T, :], ps_a[:, :], ACT.Identity, scale=chn[:, k:k + 1],
                               bias=chn[:, C_CB + T:C_CB + T + 1]).then_inc(s_cva, 1)

            def softplus(c, T, k):
                if k == 0:
                    act.wait_ge(s_ta, 9 * c + 5 + T + 1)
                    if T == 0:
                        nonneg(act, s_re, 8 * c)
                    act.activation(val[:, 0, T, :], ps_a[:, :], ACT.Identity,
                                   bias=chn[:, C_BDT + T:C_BDT + T + 1]).then_inc(s_spa, 1)
                else:
                    act.wait_ge(s_spa, 8 * c + 4 * T + k)
                if k == 1:
                    nonneg(act, s_dt, 2 * c + T)
                    act.activation(soft[:, :], val[:, 0, T, :], ACT.Abs).then_inc(s_spa, 1)
                if k == 2:
                    act.activation(soft[:, :], soft[:, :], ACT.Exp, scale=-1.0).then_inc(s_spa, 1)
                if k == 3:
                    act.activation(soft[:, :], soft[:, :], ACT.Ln, bias=1.0).then_inc(s_spa, 1)

            def relu(c, e, half):
                act.wait_ge(s_l1, 2 * E * c + 2 * e + half + 1)
                if e >= 2:
                    act.wait_ge(s_l2, E * c + e - 1)
                act.activation(hid[:, e % 2, half, :], ps_c[0][:, :], ACT.Relu,
                               bias=b1[:, 2 * e + half:2 * e + half + 1]).then_inc(s_re1, 1)

            def stage_c(c, i):
                if i == ACT_AT["norm2"]:
                    act.wait_ge(s_rs2, 2 * c + 2)
                    normalize(x2, rstdc, shiftc, xn2, s_xn2)
                if i == ACT_AT["turn2"]:
                    act.wait_ge(s_t2, c + 1)
                    act.activation(xn2T[:, :], ps_c[0][:, :], ACT.Copy).then_inc(s_x2T, 1)
                if i == ACT_AT["expo"]:
                    act.wait_ge(s_rt, R_STEPS * c + 12)
                    act.activation(expo[:, :, :], shifted[:, :, :], ACT.Exp).then_inc(s_ex, 1)
                if i == ACT_AT["gates"]:
                    act.wait_ge(s_gt, c + 1)
                    act.activation(gT[:, :], ps_a[0:E, :], ACT.Copy).then_inc(s_gT, 1)
                for unit in range(2 * E):
                    if i == RELU_AT[unit]:
                        relu(c, unit // 2, unit % 2)

            def step(ca, cb, cc, cd, par):
                if ca is not None and not (isinstance(ca, int) and ca == 0):
                    act.wait_ge(s_xn, TT * ca)
                    rows = x[bass.ds(ca * TOK, TOK), :].rearrange("(t p) c -> p t c", p=P)
                    act.dma_start(xt[:, :, :], rows).then_inc(s_x, 16)
                for i in range(DI):
                    if cb is not None and i + LOOK - 1 < DI:
                        decays(cb, i + LOOK - 1)
                    if ca is not None and i + LOOK - 1 >= DI:
                        decays(ca, i + LOOK - 1 - DI)
                    if cd is not None:
                        stage_c(cd, DI + i)
                    if cc is not None:
                        stage_c(cc, i)
                    if ca is not None:
                        if i == ACT_AT["norm"]:
                            act.wait_ge(s_rs, 2 * ca + 2)
                            nonneg(act, s_ta, 9 * (ca - 1) + 1)
                            normalize(xt, rstd, shift, xn, s_xn)
                        if i == ACT_AT["xnT"]:
                            a_copy(xnT[:, :], 0, ca, s_xnT)
                        if i == ACT_AT["xin0"]:
                            act.wait_ge(s_pad, ca + 1)
                            a_copy(xin[:, 0, TAPS - 1:], 1, ca, s_xin)
                            last_tap(ca, 0)
                        if i == ACT_AT["xin1"]:
                            a_copy(xin[:, 1, TAPS - 1:], 2, ca, s_xin)
                            last_tap(ca, 1)
                        for T in range(NT):
                            if i == ACT_AT[f"z{T}"]:
                                if T == 0:
                                    nonneg(act, s_yg, 2 * (ca - 1))
                                a_copy(sz[:, par, T, :], 3 + T, ca, s_z)
                        if i == ACT_AT["silu"]:
                            for T in range(NT):
                                act.wait_ge(s_z, 2 * ca + T + 1)
                                act.activation(sz[:, par, T, :], sz[:, par, T, :], ACT.Silu).then_inc(s_sz, 1)
                            for T in range(NT):
                                act.wait_ge(s_cv, 6 * ca + 5 + T)
                                act.activation(xc[:, par, T, :], cv[:, T, :], ACT.Silu).then_inc(s_xc, 1)
                            act.preload_act_table_set("natural_log_exp_and_others")
                        for T in range(NT):
                            for k in range(4):
                                if i == ACT_AT[f"sp{T}{k}"]:
                                    softplus(ca, T, k)
                        if i == ACT_AT["b"]:
                            nonneg(act, s_pr, DI * (ca - 1))
                            a_copy(bc[:, par, 0, :], 7, ca, s_bc)
                        if i == ACT_AT["c"]:
                            a_copy(bc[:, par, 1, :], 8, ca, s_bc)
                        for T in range(NT):
                            for w in range(2):
                                if i == ACT_AT[f"pc{T}{w}"]:
                                    if w == 0:
                                        nonneg(act, s_sk[T], 16 * 12 * ca)
                                        act.wait_ge(s_dt, 2 * ca + T + 1)
                                    else:
                                        act.wait_ge(s_dx, 2 * ca + T + 1)
                                    act.activation(pieces[:, T, 0, w, :], val[:, w, T, :], ACT.Copy).then_inc(s_pc, 1)
                            for w in range(2):
                                if i == ACT_AT[f"pc{T}{2 + w}"]:
                                    act.wait_ge(s_re, 8 * ca + 4 * T + w + 1)
                                    act.activation(pieces[:, T, 1, w, :], val[:, w, T, :], ACT.Copy).then_inc(s_pc, 1)

            act.wait_ge(s_aneg, 1)
            steps(act, step)

        @block.tensor
        def _(pe):
            pe.wait_ge(s_w1, 16 * SMALL)
            pe.wait_ge(s_sel, 1)
            pe.wait_ge(s_wmix, 1)

            def bcast(c, i, w, par):
                n = DI * c + i
                T, q, s = channel(i)
                if w == 0:
                    nonneg(pe, s_de, n - 1)
                    bank, done = ps_dt[i % 2], s_bdt
                else:
                    nonneg(pe, s_dr, n - 1)
                    bank, done = ps_dx[i % 2], s_bdx
                pe.matmul(bank[:, :], sel[:, q, :], stack[:, par, T, s, w, :],
                          start=True, stop=True).then_inc(done, 1)

            def y_group(c, g):
                q = g % NQ
                pe.wait_ge(s_pr, DI * c + NS * g + NS)
                if q == 0:
                    nonneg(pe, s_ys, 2 * c + g // NQ)
                for s in range(NS):
                    mm = pe.matmul(ps_y[32 * s:32 * s + 32, :], ysel[:, q, :], prod[:, n_mod(NS * g + s), :],
                                   start=(q == 0), stop=(q == NQ - 1))
                mm.then_inc(s_y, 1)

            def project(weights, rhs):
                for j, (a, b) in enumerate(zip(weights, rhs)):
                    mm = pe.matmul(ps_a[:, :], a, b, start=(j == 0), stop=(j == len(weights) - 1))
                mm.then_inc(s_ta, 1)

            def stage_a(c, i, par):
                xcs = [xc[:, par, T, :] for T in range(NT)]
                if i == PE_AT["turn"]:
                    nonneg(pe, s_bc, 2 * c)
                    nonneg(pe, s_ai, c - 1)
                    pe.wait_ge(s_xn, TT * (c + 1))
                    for t in range(TT):
                        mm = pe.transpose(ps_a[:, t * P:(t + 1) * P], xn[:, t, :], ident)
                    mm.then_inc(s_ta, 1)
                if i == PE_AT["in0"]:
                    pe.wait_ge(s_xnT, c + 1)
                    project([win2[:, 0, :]], [xnT[:, :]])
                if i == PE_AT["in1"]:
                    pe.wait_ge(s_cva, 2 * c + 1)
                    project([win2[:, 1, :]], [xnT[:, :]])
                if i == PE_AT["in2"]:
                    pe.wait_ge(s_cva, 2 * c + 2)
                    project([win2[:, 2, :]], [xnT[:, :]])
                if i == PE_AT["in3"]:
                    pe.wait_ge(s_z, 2 * c + 1)
                    project([win2[:, 3, :]], [xnT[:, :]])
                if i == PE_AT["dt0"]:
                    pe.wait_ge(s_z, 2 * c + 2)
                    pe.wait_ge(s_xc, 2 * c + 2)
                    project([wdt2[:, T, 0, :] for T in range(NT)], xcs)
                if i == PE_AT["dt1"]:
                    pe.wait_ge(s_spa, 8 * c + 1)
                    project([wdt2[:, T, 1, :] for T in range(NT)], xcs)
                if i == PE_AT["b"]:
                    pe.wait_ge(s_spa, 8 * c + 5)
                    project([wbc2[:, 0, T, :] for T in range(NT)], xcs)
                if i == PE_AT["c"]:
                    pe.wait_ge(s_bc, 2 * c + 1)
                    project([wbc2[:, 1, T, :] for T in range(NT)], xcs)

            def hidden(c, e, half):
                if (e, half) == (0, 0):
                    pe.wait_ge(s_x2T, c + 1)
                else:
                    pe.wait_ge(s_re1, 2 * E * c + 2 * e + half)
                pe.matmul(ps_c[0][:, :], w1[:, e, half * P:(half + 1) * P], xn2T[:, :],
                          start=True, stop=True).then_inc(s_l1, 1)

            def expert_out(c, e, part):
                if part == 0:
                    pe.wait_ge(s_re1, 2 * E * c + 2 * e + 2)
                    if e == 0:
                        pe.wait_ge(s_rt, R_STEPS * c + 1)
                    else:
                        pe.wait_ge(s_ad, 1 + E * c + e)
                for t in range(2 * part, 2 * part + 2):
                    for half in range(2):
                        mm = pe.matmul(ps_c[1][:, t * P:(t + 1) * P], hid[:, e % 2, half, t * P:(t + 1) * P],
                                       w2[:, e, half, :], start=(half == 0), stop=(half == 1))
                if part == 1:
                    mm.then_inc(s_l2, 1)

            def stage_c(c, i):
                if i == PE_AT["y"]:
                    y_group(c, NR - 1)
                if i == PE_AT["out"]:
                    pe.wait_ge(s_yg, 2 * c + 2)
                    pe.wait_ge(s_ad, 1 + E * c)
                    for t in range(TT):
                        for T in range(NT):
                            mm = pe.matmul(ps_c[1][:, t * P:(t + 1) * P], yg[:, T, t * P:(t + 1) * P],
                                           wout2[:, T, :], start=(T == 0), stop=(T == NT - 1))
                    mm.then_inc(s_op, 1)
                if i == PE_AT["turn2"]:
                    pe.wait_ge(s_xn2, TT * (c + 1))
                    for t in range(TT):
                        mm = pe.transpose(ps_c[0][:, t * P:(t + 1) * P], xn2[:, t, :], ident)
                    mm.then_inc(s_t2, 1)
                if i == PE_AT["route"]:
                    pe.wait_ge(s_x2T, c + 1)
                    pe.wait_ge(s_x2, c + 1)
                    if isinstance(c, int):
                        pe.wait_ge(s_w2, 16 * FFN)
                    pe.matmul(ps_c[1][:, 0:TT * E], ones[:, :], br[:, :], start=True, stop=False)
                    for t in range(TT):
                        mm = pe.matmul(ps_c[1][:, t * E:(t + 1) * E], xn2T[:, t * P:(t + 1) * P], wr[:, :],
                                       start=False, stop=(t == TT - 1))
                    mm.then_inc(s_lo, 1)
                if i == PE_AT["gates"]:
                    pe.wait_ge(s_rt, R_STEPS * (c + 1))
                    pe.wait_ge(s_bc, a_done(c, 2, 2))
                    for t in range(TT):
                        mm = pe.matmul(ps_a[0:E, t * P:(t + 1) * P], gates[:, t, :], ident, start=True, stop=True)
                    mm.then_inc(s_gt, 1)
                if i == PE_AT["bias"]:
                    pe.wait_ge(s_gT, c + 1)
                    for t in range(TT):
                        mm = pe.matmul(ps_a[:, t * P:(t + 1) * P], gT[:, t * P:(t + 1) * P], b2[:, :],
                                       start=True, stop=True)
                    mm.then_inc(s_b2, 1)
                for unit in range(2 * E):
                    if i == HIDDEN_AT[unit]:
                        hidden(c, unit // 2, unit % 2)
                    if unit >= 2 and i == EXPERT_AT[unit - 2]:
                        expert_out(c, unit // 2 - 1, unit % 2)
                for part in range(2):
                    if i == EXPERT_AT[2 * E - 2 + part]:
                        expert_out(c, E - 1, part)

            def a_done(c, per, at):
                if isinstance(c, int) and c + 2 >= n_chunks:
                    return per * n_chunks
                return per * (c + 2) + at

            def step(ca, cb, cc, cd, par):
                bpar = 1 - par
                for i in range(DI):
                    if cb is not None:
                        if i + LOOK == DT:
                            pe.wait_ge(s_sk[1], 16 * 12 * (cb + 1))
                        if i + LOOK < DI:
                            bcast(cb, i + LOOK, 0, bpar)
                        if i + 1 < DI:
                            bcast(cb, i + 1, 1, bpar)
                        if i >= Y_AT and (i - Y_AT) % NS == 0:
                            y_group(cb, (i - Y_AT) // NS)
                    if ca is not None and i + LOOK >= DI:
                        if i + LOOK == DI:
                            pe.wait_ge(s_sk[0], 16 * 12 * (ca + 1))
                        bcast(ca, i + LOOK - DI, 0, par)
                        if i == DI - 1:
                            bcast(ca, 0, 1, par)
                    if cd is not None:
                        stage_c(cd, DI + i)
                    if cc is not None:
                        stage_c(cc, i)
                    if ca is not None:
                        stage_a(ca, i, par)

            win2 = win[:, :, :].rearrange("p (m e) h -> p m (e h)", m=4)
            wbc2 = wbc[:, :, :, :, :].rearrange("p b t h n -> p b t (h n)")
            wdt2 = wdt[:, :, :, :, :].rearrange("p k t d h -> p k t (d h)")
            wout2 = wout[:, :, :, :].rearrange("p t h i -> p t (h i)")
            steps(pe, step)

        @block.vector
        def _(dve):
            dve.wait_ge(s_w1, 16 * SMALL)
            dve.memset(ones[:, :], 1.0)
            dve.memset(minus_half[:, :], -0.5)
            dve.tensor_copy(sel[:, :, :], cst[0:96, K_SEL:K_SEL + NQ * P].rearrange("p (q m) -> p q m", q=NQ)
                            ).then_inc(s_sel, 1)
            dve.tensor_tensor(win[:, :, :], win_c[:, :].unsqueeze(2).to_broadcast([P, 4 * DT, H]),
                              head_of_in.unsqueeze(1).to_broadcast([P, 4 * DT, H]), ALU.mult)
            for T in range(NT):
                for b in range(2):
                    dve.tensor_tensor(wbc[:, b, T, :, :],
                                      wxp[:, T, 1 + N * b:1 + N * b + N].unsqueeze(1).to_broadcast([P, H, N]),
                                      head_of_ch.unsqueeze(2).to_broadcast([P, H, N]), ALU.mult)
                for T2 in range(NT):
                    dve.scalar_tensor_tensor(
                        out=wdt[:, T, T2, :, :],
                        in0=wdt_b[:, T2 * DT * H:(T2 + 1) * DT * H].rearrange("p (d h) -> p d h", h=H),
                        scalar=wxp[:, T, 0:1], in1=head_of_ch.unsqueeze(1).to_broadcast([P, DT, H]),
                        op0=ALU.mult, op1=ALU.mult)
                last = dve.tensor_tensor(
                    wout[:, T, :, :],
                    chn[:, C_WO + T * DH:C_WO + (T + 1) * DH].unsqueeze(1).to_broadcast([P, H, DH]),
                    head_of_ch.unsqueeze(2).to_broadcast([P, H, DH]), ALU.mult)
            last.then_inc(s_wmix, 1)
            dve.wait_ge(s_apos, 1)
            dve.tensor_scalar(neg_a[:, :], pos_a[:, :], -1.0, None, ALU.mult).then_inc(s_aneg, 1)
            dve.wait_ge(s_aneg, 1)
            dve.memset(both[:, :, :], 0.0).then_inc(s_ad, 1)
            dve.memset(inv[:, :], 0.0).then_inc(s_ai, 1)

            def drives(c, i, par):
                n = DI * c + i
                dve.wait_ge(s_bdx, n + 1)
                nonneg(dve, s_h, n - 3)
                dve.tensor_tensor(drive[:, i % 4, :], ps_dx[i % 2][:, :], bc[:, par, 0, :],
                                  ALU.mult).then_inc(s_dr, 1)

            def scan(c, i, par):
                n = DI * c + i
                dve.wait_ge(s_de, n + 1)
                dve.wait_ge(s_dr, n + 1)
                if i % NS == 0 and (i >= RING) == (par == 0):
                    nonneg(dve, s_pr, n - RING + NS + 1)
                else:
                    nonneg(dve, s_pr, n - RING + 1)
                initial = 0.0
                if par == 1:
                    if i % NS == 0:
                        dve.wait_ge(s_ca, carries(c, i))
                    initial = carry[:, i:i + 1]
                dve.tensor_tensor_scan(state[:, n_mod(i), :], decay[:, n_mod(i), :], drive[:, i % 4, :],
                                       initial, ALU.mult, ALU.add).then_inc(s_h, 1)

            def carries(c, i):
                return half(c, NR) + i // NS + 1

            def half(c, per):
                if isinstance(c, int):
                    return (c // 2) * per
                return (c - 1) * (per // 2)

            def stats(src, st, m, v, nm, done, c, k):
                if k == 0:
                    for t in range(TT):
                        dve.bn_stats(st[:, t, :], src[:, t, :]).then_inc(done, 1)
                if k == 1:
                    for t in range(TT):
                        dve.bn_aggr(m[:, t, :], st[:, t, :]).then_inc(done, 1)
                if k == 2:
                    dve.wait_ge(done, 10 * c + 2 * TT)
                    dve.tensor_scalar(v[:, :], m[:, :, 1], EPS, None, ALU.add).then_inc(done, 1)
                    dve.tensor_scalar(nm[:, :], m[:, :, 0], -1.0, None, ALU.mult).then_inc(done, 1)

            def conv(c, k):
                for T in range(NT):
                    if k == 0:
                        dve.wait_ge(s_cva, 2 * c + T + 1)
                    else:
                        dve.wait_ge(s_cv, 6 * c + 2 * k + T - 1)
                    dve.scalar_tensor_tensor(out=cv[:, T, :], in0=xin[:, T, k:k + TOK],
                                             scalar=chn[:, C_CW + TAPS * T + k:C_CW + TAPS * T + k + 1],
                                             in1=cv[:, T, :], op0=ALU.mult, op1=ALU.add).then_inc(s_cv, 1)

            def softplus(c, T):
                dve.wait_ge(s_spa, 8 * c + 4 * T + 4)
                dve.scalar_tensor_tensor(out=val[:, 0, T, :], in0=val[:, 0, T, :], scalar=0.0, in1=soft[:, :],
                                         op0=ALU.max, op1=ALU.add).then_inc(s_dt, 1)

            def skip(c, T, par):
                dve.wait_ge(s_y, NR * c + NQ * (T + 1))
                if T == 0:
                    nonneg(dve, s_op, c)
                dve.scalar_tensor_tensor(out=yg[:, T, :], in0=xc[:, par, T, :],
                                         scalar=chn[:, C_DP + T:C_DP + T + 1], in1=ps_y[:, :],
                                         op0=ALU.mult, op1=ALU.add).then_inc(s_ys, 1)

            def over_e(ap):
                return ap.unsqueeze(2).to_broadcast([P, TT, E])

            def routing(c, k):
                base = R_STEPS * c
                if k > 0:
                    dve.wait_ge(s_rt, base + k)
                if k == 0:
                    dve.wait_ge(s_lo, c + 1)
                    op = dve.tensor_copy(lg[:, :, :], ps_c[1][:, 0:TT * E].rearrange("p (t e) -> p t e", t=TT))
                elif k == 1:
                    op = dve.tensor_reduce(top[:, 0, :], lg[:, :, :], AX_X, ALU.max)
                elif k == 2:
                    op = dve.tensor_tensor(eq[:, 0, :, :], lg[:, :, :], over_e(top[:, 0, :]), ALU.is_equal)
                elif k == 3:
                    op = dve.tensor_tensor(eq[:, 0, :, :], eq[:, 0, :, :], order, ALU.mult)
                elif k == 4:
                    op = dve.tensor_reduce(first[:, 0, :], eq[:, 0, :, :], AX_X, ALU.max)
                elif k == 5:
                    op = dve.tensor_tensor(pick[:, 0, :, :], eq[:, 0, :, :], over_e(first[:, 0, :]), ALU.is_equal)
                elif k == 6:
                    op = dve.scalar_tensor_tensor(out=lg2[:, :, :], in0=pick[:, 0, :, :], scalar=-BIG,
                                                  in1=lg[:, :, :], op0=ALU.mult, op1=ALU.add)
                elif k == 7:
                    op = dve.tensor_reduce(top[:, 1, :], lg2[:, :, :], AX_X, ALU.max)
                elif k == 8:
                    op = dve.tensor_tensor(eq[:, 1, :, :], lg2[:, :, :], over_e(top[:, 1, :]), ALU.is_equal)
                elif k == 9:
                    op = dve.tensor_tensor(eq[:, 1, :, :], eq[:, 1, :, :], order, ALU.mult)
                elif k == 10:
                    op = dve.tensor_reduce(first[:, 1, :], eq[:, 1, :, :], AX_X, ALU.max)
                elif k == 11:
                    op = dve.tensor_tensor(shifted[:, :, :], lg[:, :, :], over_e(top[:, 0, :]), ALU.subtract)
                elif k == 12:
                    op = dve.tensor_tensor(pick[:, 1, :, :], eq[:, 1, :, :], over_e(first[:, 1, :]), ALU.is_equal)
                elif k == 13:
                    op = dve.tensor_tensor(both[:, :, :], pick[:, 0, :, :], pick[:, 1, :, :], ALU.add)
                elif k == 14:
                    dve.wait_ge(s_ex, c + 1)
                    op = dve.tensor_tensor(masked[:, :, :], expo[:, :, :], both[:, :, :], ALU.mult)
                elif k == 15:
                    op = dve.tensor_reduce(total[:, :], masked[:, :, :], AX_X, ALU.add)
                elif k == 16:
                    op = dve.reciprocal(inv[:, :], total[:, :])
                elif k == 17:
                    op = dve.tensor_tensor(gates[:, :, :], masked[:, :, :], over_e(inv[:, :]), ALU.mult)
                op.then_inc(s_rt, 1)

            def add_expert(c, e):
                dve.wait_ge(s_l2, E * c + e + 1)
                if e == 0:
                    dve.wait_ge(s_rt, R_STEPS * (c + 1))
                    nonneg(dve, s_out, 16 * c)
                    before = x2
                else:
                    dve.wait_ge(s_ad, 1 + E * c + e)
                    before = acc
                if e == EXPERTS_BEFORE_BIAS:
                    dve.wait_ge(s_ai, c + 2)
                for t in range(TT):
                    op = dve.scalar_tensor_tensor(out=acc[:, t, :], in0=ps_c[1][:, t * P:(t + 1) * P],
                                                  scalar=gates[:, t, e:e + 1], in1=before[:, t, :],
                                                  op0=ALU.mult, op1=ALU.add)
                op.then_inc(s_ad, 1)

            def add_bias(c):
                dve.wait_ge(s_b2, c + 1)
                dve.wait_ge(s_ad, 1 + E * c + EXPERTS_BEFORE_BIAS)
                dve.tensor_tensor(acc[:, :, :], ps_a[:, :].rearrange("p (t d) -> p t d", t=TT),
                                  acc[:, :, :], ALU.add).then_inc(s_ai, 1)

            def stage_a(c, j, par):
                if j == DVE_AT["stat0"]:
                    dve.wait_ge(s_x, 16 * (c + 1))
                    stats(xt, st6, mv, var, neg_m, s_st, c, 0)
                if j == DVE_AT["stat1"]:
                    stats(xt, st6, mv, var, neg_m, s_st, c, 1)
                if j == DVE_AT["stat2"]:
                    stats(xt, st6, mv, var, neg_m, s_st, c, 2)
                if j == DVE_AT["pad"]:
                    nonneg(dve, s_cv, 6 * c)
                    if par == 0:
                        dve.memset(xin[:, :, 0:TAPS - 1], 0.0).then_inc(s_pad, 1)
                    else:
                        dve.tensor_copy(xin[:, :, 0:TAPS - 1], xin[:, :, TOK:TOK + TAPS - 1]).then_inc(s_pad, 1)
                for k in range(TAPS - 1):
                    if j == DVE_AT[f"conv{k}"]:
                        if k == 0:
                            dve.wait_ge(s_pad, c + 1)
                        conv(c, k)
                for T in range(NT):
                    if j == DVE_AT[f"dt{T}"]:
                        softplus(c, T)

            def stage_c(c, j, par):
                if j == DVE_AT["skip1"]:
                    skip(c, 1, par)
                if j == DVE_AT["x2"]:
                    dve.wait_ge(s_op, c + 1)
                    dve.wait_ge(s_xr, 16 * (c + 1))
                    dve.tensor_tensor(x2[:, :, :], ps_c[1][:, :].rearrange("p (t d) -> p t d", t=TT),
                                      xres[:, :, :], ALU.add).then_inc(s_x2, 1)
                if j == DVE_AT["cstat0"]:
                    dve.wait_ge(s_x2, c + 1)
                    stats(x2, st6c, mvc, varc, neg_mc, s_st2, c, 0)
                if j == DVE_AT["cstat1"]:
                    stats(x2, st6c, mvc, varc, neg_mc, s_st2, c, 1)
                if j == DVE_AT["cstat2"]:
                    stats(x2, st6c, mvc, varc, neg_mc, s_st2, c, 2)
                for k in range(R_STEPS):
                    if j == ROUTE_AT[k]:
                        routing(c, k)
                if j == DVE_AT["bias"]:
                    add_bias(c)
                for e in range(E):
                    if j == ADD_AT[e]:
                        add_expert(c, e)

            def step(ca, cb, cc, cd, par):
                bpar = 1 - par
                for j in range(2 * DI):
                    i = j // 2
                    if ca is not None and j == DVE_AT["stat1"]:
                        dve.wait_ge(s_st, 10 * ca + TT)
                    if cc is not None and j == DVE_AT["cstat1"]:
                        dve.wait_ge(s_st2, 10 * cc + TT)
                    if cb is not None:
                        if j % 2 == 0 and i + 1 < DI:
                            drives(cb, i + 1, bpar)
                        if j % 2 == 1:
                            scan(cb, i, bpar)
                        if j == DVE_AT["skip0"]:
                            skip(cb, 0, bpar)
                    if ca is not None and j == 2 * DI - 2:
                        dve.wait_ge(s_bc, 2 * ca + 1)
                        drives(ca, 0, par)
                    if cd is not None:
                        stage_c(cd, 2 * DI + j, 1 - par)
                    if cc is not None:
                        stage_c(cc, j, par)
                    if ca is not None:
                        stage_a(ca, j, par)

            steps(dve, step)


def n_mod(i):
    return i % RING


def kernel(L0_attn_x, L0_attn_W_in, L0_attn_conv_w, L0_attn_conv_b, L0_attn_W_xp, L0_attn_W_dt,
           L0_attn_b_dt, L0_attn_A_log, L0_attn_Dp, L0_attn_W_out, L0_ffn_Wr, L0_ffn_br, L0_ffn_W1,
           L0_ffn_b1, L0_ffn_W2, L0_ffn_b2):
    import numpy as np
    import concourse.bacc as bacc
    from concourse.bass_utils import run_bass_kernel_spmd

    c = np.zeros((P, K_END), np.float32)
    rows = np.arange(P)
    c[rows, K_ID + rows] = 1
    for q in range(NQ):
        for h in range(H):
            for piece in range(3):
                c[32 * piece + 8 * q + h, K_SEL + P * q + N * h:K_SEL + P * q + N * h + N] = 1
            c[N * h:N * h + N, K_YSEL + 32 * q + 8 * q + h] = 1
    c[rows, K_HM1 + rows // DH] = 1
    c[rows, K_HM2 + rows % H] = 1
    c[:, K_ORD:K_END] = np.tile(np.arange(E, 0, -1), TT)

    def by_channel(a):
        a = np.asarray(a).reshape((H, NT, DT) + a.shape[2:])
        a = np.moveaxis(a, (2, 0, 1), (0, 1, 2))
        return np.ascontiguousarray(a).reshape(P, -1)

    chan = np.concatenate([by_channel(a) for a in (L0_attn_conv_w, L0_attn_conv_b, L0_attn_W_xp,
                                                   L0_attn_b_dt, L0_attn_Dp, L0_attn_W_out)], axis=1)
    arrays = {
        "x_in": np.ascontiguousarray(L0_attn_x).reshape(-1, P),
        "consts_in": c,
        "chan_in": chan,
        "w_in_in": np.ascontiguousarray(L0_attn_W_in).reshape(P, 4 * DT),
        "w_dt_in": np.ascontiguousarray(np.transpose(np.asarray(L0_attn_W_dt)[:, 0, :], (1, 0))).reshape(-1),
        "a_log_in": np.ascontiguousarray(np.transpose(np.asarray(L0_attn_A_log), (0, 2, 1))).reshape(P, DI),
        "w_r_in": np.ascontiguousarray(L0_ffn_Wr),
        "b_r_in": np.tile(np.asarray(L0_ffn_br), TT).reshape(1, TT * E),
        "w_1_in": np.ascontiguousarray(L0_ffn_W1),
        "b_1_in": np.ascontiguousarray(np.transpose(np.asarray(L0_ffn_b1).reshape(2 * E, P), (1, 0))),
        "w_2_in": np.ascontiguousarray(L0_ffn_W2),
        "b_2_in": np.ascontiguousarray(L0_ffn_b2),
    }
    nc = bacc.Bacc("TRN2", target_bir_lowering=False, num_devices=1)
    args = [nc.dram_tensor(name, a.shape, mybir.dt.from_np(a.dtype), kind="ExternalInput").ap()
            for name, a in arrays.items()]
    shape = tuple(L0_attn_x.shape)
    out = nc.dram_tensor("block_out", (shape[0] * shape[1], P), F32, kind="ExternalOutput").ap()
    build(nc, *args, out)
    r = run_bass_kernel_spmd(nc, [arrays], core_ids=[0])
    return np.asarray(r.results[0]["block_out"]).reshape(shape)
```
